# Optimizing a Trainium2 kernel written in Bass

```python
import numpy as np
import jax
import jax.numpy as jnp

def _softmax(x, axis=-1):
    return jax.nn.softmax(x, axis=axis)

def _gelu(x):
    return jax.nn.gelu(x, approximate=True)

def _silu(x):
    return jax.nn.silu(x)

def _sigmoid(x):
    return jax.nn.sigmoid(x)

def _layernorm(x, axis=-1, eps=1e-05):
    m = jnp.mean(x, axis=axis, keepdims=True)
    v = jnp.var(x, axis=axis, keepdims=True)
    return (x - m) / jnp.sqrt(v + eps)

def _scatter_add(tgt, idx, src, axis=0):
    return tgt.at[idx].add(src)

def _segment_sum(src, seg, n):
    return jax.ops.segment_sum(src, seg, n)
kernel_name = 'mk_seq_preln_d1_jaxref_r4_a4c478'

def setup_inputs(seed: int=0):
    np.random.seed(seed)
    _w = jnp.asarray

    def _L0_attn_setup():
        import jax, jax.numpy as jnp
        from jax import lax
        import numpy as np
        import math
        EMBED_DIM = 256
        NUM_HEADS = 16
        REDUCTION = 2
        key = jax.random.key(seed)
        ks = jax.random.split(key, 11)
        B, N, C = (2, 1024, EMBED_DIM)
        s = 1.0 / math.sqrt(C)
        return {'x': jax.random.normal(ks[0], (B, N, C), jnp.float32), 'q_w': jax.random.normal(ks[1], (C, C), jnp.float32) * s, 'q_b': jax.random.normal(ks[2], (C,), jnp.float32) * s, 'k_w': jax.random.normal(ks[3], (C, C), jnp.float32) * s, 'k_b': jax.random.normal(ks[4], (C,), jnp.float32) * s, 'v_w': jax.random.normal(ks[5], (C, C), jnp.float32) * s, 'v_b': jax.random.normal(ks[6], (C,), jnp.float32) * s, 'conv_w': jax.random.normal(ks[7], (C, 1, 3), jnp.float32) * 0.5, 'conv_b': jax.random.normal(ks[8], (C,), jnp.float32) * 0.1, 'out_w': jax.random.normal(ks[9], (C, C), jnp.float32) * s, 'out_b': jax.random.normal(ks[10], (C,), jnp.float32) * s}
    _L0_attn_in = _L0_attn_setup()

    def _L0_ffn_setup():
        import jax, jax.numpy as jnp
        import numpy as np

        def _bitlinear(x, w_latent):
            scale = jax.lax.stop_gradient(jnp.clip(jnp.mean(jnp.abs(w_latent), axis=1, keepdims=True), 1e-05, None))
            tern = jnp.clip(jnp.round(w_latent / scale), -1.0, 1.0)
            w = w_latent + jax.lax.stop_gradient(tern - w_latent)
            return x @ (w * scale).T
        key = jax.random.key(seed)
        ks = jax.random.split(key, 6)
        dim, hidden, rank = (256, 1024, 16)
        B, S = (4, 1024)
        x = jax.random.normal(ks[0], (B, S, dim), dtype=jnp.float32)
        w_fc = 0.02 * jax.random.normal(ks[1], (hidden, dim), dtype=jnp.float32)
        w_proj = 0.02 * jax.random.normal(ks[2], (dim, hidden), dtype=jnp.float32)
        u = 0.02 * jax.random.normal(ks[3], (hidden, rank), dtype=jnp.float32)
        v = 0.02 * jax.random.normal(ks[4], (rank, dim), dtype=jnp.float32)
        fast_b = jax.random.normal(ks[5], (rank, rank), dtype=jnp.float32)
        gate = jnp.float32(0.05)
        return {'x': x, 'fast_b': fast_b, 'w_fc': w_fc, 'w_proj': w_proj, 'u': u, 'v': v, 'gate': gate}
    _L0_ffn_in = _L0_ffn_setup()
    _d = {'L0_attn_x': _L0_attn_in['x'], 'L0_attn_q_w': _L0_attn_in['q_w'], 'L0_attn_q_b': _L0_attn_in['q_b'], 'L0_attn_k_w': _L0_attn_in['k_w'], 'L0_attn_k_b': _L0_attn_in['k_b'], 'L0_attn_v_w': _L0_attn_in['v_w'], 'L0_attn_v_b': _L0_attn_in['v_b'], 'L0_attn_conv_w': _L0_attn_in['conv_w'], 'L0_attn_conv_b': _L0_attn_in['conv_b'], 'L0_attn_out_w': _L0_attn_in['out_w'], 'L0_attn_out_b': _L0_attn_in['out_b'], 'L0_ffn_fast_b': _L0_ffn_in['fast_b'], 'L0_ffn_w_fc': _L0_ffn_in['w_fc'], 'L0_ffn_w_proj': _L0_ffn_in['w_proj'], 'L0_ffn_u': _L0_ffn_in['u'], 'L0_ffn_v': _L0_ffn_in['v'], 'L0_ffn_gate': _L0_ffn_in['gate']}
    _x0 = _d['L0_attn_x']
    _d['L0_attn_x'] = jax.random.normal(jax.random.fold_in(jax.random.key(seed), 1), (1, 4096, 256), dtype=_x0.dtype)
    del _x0
    return _d

def reference(L0_attn_x, L0_attn_q_w, L0_attn_q_b, L0_attn_k_w, L0_attn_k_b, L0_attn_v_w, L0_attn_v_b, L0_attn_conv_w, L0_attn_conv_b, L0_attn_out_w, L0_attn_out_b, L0_ffn_fast_b, L0_ffn_w_fc, L0_ffn_w_proj, L0_ffn_u, L0_ffn_v, L0_ffn_gate):

    def _L0_attn_ref(x, q_w, q_b, k_w, k_b, v_w, v_b, conv_w, conv_b, out_w, out_b):
        import jax, jax.numpy as jnp
        from jax import lax
        import numpy as np
        import math
        EMBED_DIM = 256
        NUM_HEADS = 16
        REDUCTION = 2
        B, N, C = x.shape
        H = NUM_HEADS
        D = C // H
        scale = 1.0 / math.sqrt(D)
        q = x @ q_w.T + q_b
        xd = jnp.transpose(x, (0, 2, 1))
        xd = lax.conv_general_dilated(xd, conv_w, window_strides=(REDUCTION,), padding=[(1, 1)], feature_group_count=C, dimension_numbers=('NCH', 'OIH', 'NCH'))
        xd = xd + conv_b[None, :, None]
        xd = jnp.transpose(xd, (0, 2, 1))
        k = xd @ k_w.T + k_b
        v = xd @ v_w.T + v_b
        Nk = k.shape[1]
        q = q.reshape(B, N, H, D).transpose(0, 2, 1, 3)
        k = k.reshape(B, Nk, H, D).transpose(0, 2, 1, 3)
        v = v.reshape(B, Nk, H, D).transpose(0, 2, 1, 3)
        att = jnp.einsum('bhnd,bhmd->bhnm', q, k) * scale
        att = jax.nn.softmax(att, axis=-1)
        out = jnp.einsum('bhnm,bhmd->bhnd', att, v)
        out = out.transpose(0, 2, 1, 3).reshape(B, N, C)
        return out @ out_w.T + out_b

    def _L0_ffn_ref(x, fast_b, w_fc, w_proj, u, v, gate):
        import jax, jax.numpy as jnp
        import numpy as np

        def _bitlinear(x, w_latent):
            scale = jax.lax.stop_gradient(jnp.clip(jnp.mean(jnp.abs(w_latent), axis=1, keepdims=True), 1e-05, None))
            tern = jnp.clip(jnp.round(w_latent / scale), -1.0, 1.0)
            w = w_latent + jax.lax.stop_gradient(tern - w_latent)
            return x @ (w * scale).T
        h = _bitlinear(x, w_fc) + gate * (x @ v.T @ fast_b.T @ u.T)
        r = jnp.maximum(h, 0.0)
        return _bitlinear(r * r, w_proj)
    x = L0_attn_x
    x = x + _L0_attn_ref(_layernorm(x, axis=-1), L0_attn_q_w, L0_attn_q_b, L0_attn_k_w, L0_attn_k_b, L0_attn_v_w, L0_attn_v_b, L0_attn_conv_w, L0_attn_conv_b, L0_attn_out_w, L0_attn_out_b)
    x = x + _L0_ffn_ref(_layernorm(x, axis=-1), L0_ffn_fast_b, L0_ffn_w_fc, L0_ffn_w_proj, L0_ffn_u, L0_ffn_v, L0_ffn_gate)
    return x

_drawn_inputs = setup_inputs


def setup_inputs(seed=0):
    import zlib

    import numpy as np

    out = dict(_drawn_inputs(seed))
    spreads = {}
    factors = {'L0_attn_q_b': 8.0,
     'L0_attn_k_b': 8.0,
     'L0_ffn_fast_b': 8.0,
     'L0_ffn_u': 8.0,
     'L0_ffn_v': 8.0}
    for name, (base, spread) in spreads.items():
        noise = np.random.default_rng([zlib.crc32(name.encode()), seed]).standard_normal(out[name].shape)
        drawn = base * np.exp(spread * noise) if base else spread * noise
        out[name] = jnp.asarray(drawn.astype(out[name].dtype))
    for name, factor in factors.items():
        out[name] = (out[name] * factor).astype(out[name].dtype)
    return out
```

```python
import struct
from contextlib import ExitStack

import concourse.bass as bass
from concourse import mybir

F32 = mybir.dt.float32
BF16 = mybir.dt.bfloat16
ALU = mybir.AluOpType
ACT = mybir.ActivationFunctionType
AX_X = mybir.AxisListType.X

P = 128
BANK = 512
LN_EPS = 1e-5
SCALE_MIN = 1e-5
PARTS = 3
Q_PART = (0, 0, 0, 1, 1, 2)
K_PART = (0, 1, 2, 0, 1, 0)
MINUS_ONES = struct.unpack("<f", struct.pack("<I", 0xBF80BF80))[0]


def build_layer(nc, x, q_wT, q_b, k_wT, k_b, v_wT, v_b, conv_w, conv_b, o_wT, o_b,
                fast_bT, w_fc, w_proj, uT, v_lr, gate, ident_f, out):
    N, C = x.shape
    NK = N // 2
    D = 16
    H = C // D
    KC = C // P
    F = w_fc.shape[0]
    FT = F // P
    R = uT.shape[0]
    G = 4
    NG = H // G
    CH = BANK
    NCH = N // CH
    QT = CH // P
    NB = NCH * NG
    KT = NK // P
    SPLIT = len(Q_PART) * D
    ROWS = SPLIT + PARTS
    VW = D + 1
    SC = 1024
    NSC = N // SC
    SK = SC // 2
    ST = SC // P
    LEAD = 4
    SLOTS = 4
    RING = 2 * G
    SCALE = float(D) ** -0.5

    with ExitStack() as ctx:
        queue = {name: [] for name in ("tensor", "vector", "scalar", "gpsimd", "sync")}

        def counter(name):
            return {"sem": ctx.enter_context(nc.semaphore(name)), "count": 0}

        def do(engine, issue, sig=None, by=1):
            queue[engine].append((issue, sig, by))
            if sig is None:
                return None
            sig["count"] += by
            return sig["sem"], sig["count"]

        def wait(engine, *marks):
            for mark in marks:
                if mark is not None:
                    queue[engine].append((lambda e, m=mark: e.wait_ge(m[0], m[1]), None, 0))

        def issue_all(name, e):
            for issue, sig, by in queue[name]:
                ins = issue(e)
                if sig is not None:
                    ins.then_inc(sig["sem"], by)

        def sb(name, shape, dt=F32):
            return ctx.enter_context(nc.sbuf_tensor(name, shape, dt))

        keys = sb("keys", [ROWS, H, NK], BF16)
        queries = sb("queries", [ROWS, SLOTS, G, CH], BF16)
        xnT = sb("xnT", [P, KC, 1 + N])
        values = sb("values", [P, KT, H, VW])
        ring = sb("ring", [P, RING * CH])
        probs = [ring[:, i * CH:(i + 1) * CH] for i in range(RING)]
        xs = [ring[:, i * ST * C:(i + 1) * ST * C].rearrange("p (t c) -> p t c", t=ST) for i in range(2)]
        qw = sb("qw", [P, KC, C])
        ow = sb("ow", [P, KC, C])
        w1 = sb("w1", [P, KC, F])
        kw, vw = w1[:, 0, 0:KC * C].rearrange("p (k c) -> p k c", k=KC), \
            w1[:, 1, 0:KC * C].rearrange("p (k c) -> p k c", k=KC)
        w2 = sb("w2", [P, FT, C])
        full = sb("full", [P, CH])
        rest = sb("rest", [P, CH])
        part = [sb(f"part{j}", [P, CH], BF16) for j in range(PARTS)]
        r2 = sb("r2", [P, FT * C])
        xd = r2[:, 0:KC * SK].rearrange("p (k n) -> p k n", k=KC)
        oT = sb("oT", [P, CH])
        attn = sb("attn", [P, QT, C])
        attnT = sb("attnT", [P, KC, CH])
        x1 = sb("x1", [P, QT, C])
        relu = sb("relu", [P, BANK])
        maxes = sb("maxes", [P, 2, QT, G, 2])
        maxs = sb("maxs", [P, QT, G])
        maxr = sb("maxr", [P, QT, G])
        mparts = sb("mparts", [P, QT, P], BF16)
        rden = sb("rden", [P, QT, G])
        stats = sb("stats", [P, ST, 6])
        meanvar = sb("meanvar", [P, ST, 2])
        rstd = sb("rstd", [P, ST])
        shift = sb("shift", [P, ST])
        half = sb("half", [P, ST])
        ident = sb("ident", [P, P])
        identb = sb("identb", [P, P], BF16)
        ones_row = sb("ones_row", [1, P])
        vb_row = sb("vb_row", [1, C])
        ob_all = sb("ob_all", [P, C])
        qb = sb("qb", [P, KC])
        qbs = sb("qbs", [P, KC])
        kb = sb("kb", [P, KC])
        cw = sb("cw", [P, KC, 3])
        cb = sb("cb", [P, KC])
        fbT = sb("fbT", [R, R])
        vlr = sb("vlr", [R, C])
        uTs = sb("uTs", [R, F])
        gcol = sb("gcol", [R, 1])
        low = sb("low", [R, C])
        wstat = sb("wstat", [P, 4])

        psum = [ctx.enter_context(nc.psum_tensor(f"bank{i}", [P, BANK], F32)) for i in range(4, 8)]
        wide = [ctx.enter_context(nc.psum_tensor(f"wide{i}", [P, 2 * BANK], F32)) for i in range(2)]
        score_bank = psum[0:2]
        pv_bank, misc_bank = psum[2], psum[3]

        k_parts = nc.dram_tensor("k_parts", [PARTS, C, NK], BF16).ap()
        q_parts = nc.dram_tensor("q_parts", [2, PARTS, P, CH], BF16).ap()

        s_const = counter("s_const")
        s_const2 = counter("s_const2")
        s_x = [counter(f"s_x{i}") for i in range(NSC)]
        s_kout = [counter(f"s_kout{i}") for i in range(2 * NSC)]
        s_kin = [counter(f"s_kin{i}") for i in range(NSC)]
        s_qout = [counter(f"s_qout{i}") for i in range(2)]
        s_qin = [counter(f"s_qin{i}") for i in range(2)]
        s_xload = counter("s_xload")
        s_store = counter("s_store")
        s_w = [counter(f"s_w{i}") for i in range(2)]
        s_pool = counter("s_pool")
        s_dve = counter("s_dve")
        s_act = counter("s_act")
        s_pe = counter("s_pe")
        s_max_scores = counter("s_max_scores")
        s_max = counter("s_max")
        s_scores = counter("s_scores")
        s_exp = counter("s_exp")
        s_pv = counter("s_pv")

        def pe(issue, sig=s_pe):
            return do("tensor", issue, sig)

        def matmul(o, lhsT, rhs, start=True, stop=True, sig=None):
            return do("tensor", lambda e: e.matmul(o, lhsT, rhs, start=start, stop=stop), sig)

        def transpose(o, i, eye, sig=None):
            return do("tensor", lambda e: e.transpose(o, i, eye), sig)

        def dve(issue, sig=s_dve):
            return do("vector", issue, sig)

        def act(o, i, func, bias=0.0, scale=1.0, sig=s_act):
            if func is None:
                return do("scalar", lambda e: e.copy(o, i), sig)
            return do("scalar", lambda e: e.activation(o, i, func, bias=bias, scale=scale), sig)

        def pool(issue, sig=s_pool):
            return do("gpsimd", issue, sig)

        def dma(o, i, sig):
            return do("sync", lambda e: e.dma_start(o, i), sig, by=16)

        free = {}
        lent = {"banks": [0, 1, 3], "next": 0}

        def borrow():
            i = lent["banks"][lent["next"] % len(lent["banks"])]
            lent["next"] += 1
            wait("tensor", free.get(i))
            return i, psum[i][:, :]

        def give_back(i, reader):
            free[i] = reader

        def load_slice(s):
            return dma(xs[s % 2], x[s * SC:(s + 1) * SC, :].rearrange("(t p) c -> p t c", p=P), s_x[s])

        def contraction(matrix):
            return matrix.rearrange("(k p) c -> p k c", p=P)

        x_loaded = {0: load_slice(0)}
        for dst, src in ((ident[:, :], ident_f), (cw[:, :, :], contraction(conv_w)), (cb[:, :], conv_b),
                         (kw, contraction(k_wT)), (kb[:, :], k_b),
                         (vw, contraction(v_wT)), (vb_row[:, :], v_b.rearrange("(a c) -> a c", a=1)),
                         (qw[:, :, :], contraction(q_wT)), (qb[:, :], q_b)):
            consts = dma(dst, src, s_const)
        x_loaded[1] = load_slice(1)
        for dst, src in ((ow[:, :, :], contraction(o_wT)),
                         (ob_all[:, :], o_b.rearrange("(a c) -> a c", a=1).broadcast_to([P, C])),
                         (fbT[:, :], fast_bT), (vlr[:, :], v_lr), (uTs[:, :], uT),
                         (gcol[:, :], gate.rearrange("(a c) -> a c", a=1).broadcast_to([R, 1]))):
            late_consts = dma(dst, src, s_const2)

        pool(lambda e: e.memset(half[:, :], -0.5))
        pool(lambda e: e.memset(ones_row[:, :], 1.0))
        pool(lambda e: e.memset(xnT[:, :, 0:1], 0.0))
        pool(lambda e: e.memset(mparts[:, :, :], 0.0))
        pool_consts = pool(lambda e: e.memset(values[:, :, :, D:VW], 1.0))
        pv_read = dve(lambda e: e.memset(pv_bank[:, :], 0.0))

        def layer_norm_stats(src, tiles, ready, stats_read):
            wait("vector", ready)
            for t in range(tiles):
                mark = dve(lambda e, t=t: e.bn_stats(stats[:, t, :], src[:, t, :]))
            wait("vector", mark, stats_read)
            for t in range(tiles):
                mark = dve(lambda e, t=t: e.bn_aggr(meanvar[:, t, :], stats[:, t, :]))
            wait("gpsimd", mark, pool_consts)
            mark = pool(lambda e: e.tensor_scalar(rstd[:, 0:tiles], meanvar[:, 0:tiles, 1], LN_EPS, None, ALU.add))
            wait("gpsimd", mark)
            mark = pool(lambda e: e.tensor_tensor(rstd[:, 0:tiles], rstd[:, 0:tiles], half[:, 0:tiles], ALU.pow))
            wait("gpsimd", mark)
            mark = pool(lambda e: e.tensor_tensor(shift[:, 0:tiles], meanvar[:, 0:tiles, 0], rstd[:, 0:tiles],
                                                  ALU.mult))
            wait("gpsimd", mark)
            return pool(lambda e: e.tensor_scalar(shift[:, 0:tiles], shift[:, 0:tiles], -1.0, None, ALU.mult))

        def normalise(engine, sig, dst, src, t):
            return do(engine, lambda e: e.tensor_scalar(dst[:, t, :], src[:, t, :], rstd[:, t:t + 1],
                                                        shift[:, t:t + 1], ALU.mult, ALU.add), sig)

        split_read = {"full": None, "parts": None}

        def split(bank, ready, bias, scale, engine, sig, store, store_sig):
            i, b = bank
            wait("scalar", ready, split_read["full"], split_read["parts"])
            act(full[:, :], b, ACT.Identity, bias=bias, scale=scale)
            first = act(part[0][:, :], b, ACT.Identity, bias=bias, scale=scale)
            give_back(i, first)
            wait(engine, first)
            m = do(engine, lambda e: e.tensor_tensor(rest[:, :], full[:, :], part[0][:, :], ALU.subtract), sig)
            wait(engine, m)
            second = do(engine, lambda e: e.tensor_copy(part[1][:, :], rest[:, :]), sig)
            wait(engine, second)
            third = do(engine, lambda e: e.tensor_tensor(part[2][:, :], rest[:, :], part[1][:, :], ALU.subtract), sig)
            for j, mark in enumerate((first, second, third)):
                wait("sync", mark)
                stored = dma(store(j), part[j][:, :], store_sig)
            split_read["full"], split_read["parts"] = third, stored
            return stored

        stats_read = None
        xs_read = [None, None]
        xd_read = None
        xnT_ready, k_ready = [], []

        def norm_slice(s):
            nonlocal stats_read
            if s >= 2:
                wait("sync", xs_read[s % 2])
                x_loaded[s] = load_slice(s)
            xb = xs[s % 2]
            mark = layer_norm_stats(xb, ST, x_loaded[s], stats_read)
            wait("vector", mark)
            for t in range(ST):
                stats_read = mark = normalise("vector", s_dve, xb, xb, t)
                if t % QT == QT - 1:
                    wait("tensor", mark, consts)
                    for k in range(KC):
                        i, bank = borrow()
                        for j in range(QT):
                            m = transpose(bank[:, j * P:(j + 1) * P],
                                          xb[:, t - QT + 1 + j, k * P:(k + 1) * P], ident[:, :], s_pe)
                        wait("scalar", m)
                        at = 1 + s * SC + (t // QT) * BANK
                        got = act(xnT[:, k, at:at + BANK], bank, None)
                        give_back(i, got)
                    xs_read[s % 2] = m
            xnT_ready.append(got)

        def keys_of_slice(s):
            nonlocal xd_read, v_ready
            wait("vector", xnT_ready[s], xd_read, consts, pool_consts)
            for k in range(KC):
                tap = [xnT[:, k, s * SC + i:s * SC + i + 2 * SK - 1:2] for i in range(3)]
                m = dve(lambda e, k=k, a=tap[1]: e.tensor_scalar(xd[:, k, :], a, cw[:, k, 1:2], cb[:, k:k + 1],
                                                                 ALU.mult, ALU.add))
                for i in (0, 2):
                    wait("vector", m)
                    m = dve(lambda e, k=k, i=i, a=tap[i]: e.scalar_tensor_tensor(
                        out=xd[:, k, :], in0=a, scalar=cw[:, k, i:i + 1], in1=xd[:, k, :],
                        op0=ALU.mult, op1=ALU.add))
            wait("tensor", m, pool_consts)
            for c in range(KC):
                bank = borrow()
                for k in range(KC):
                    m = matmul(bank[1], kw[:, k, c * P:(c + 1) * P], xd[:, k, :], start=(k == 0),
                               stop=(k == KC - 1), sig=s_pe)
                engine, sig = (("vector", s_dve), ("gpsimd", s_pool))[c]
                stored = split(bank, m, kb[:, c:c + 1], 1.0, engine, sig,
                               lambda j, c=c: k_parts[j, c * P:(c + 1) * P, s * SK:(s + 1) * SK], s_kout[2 * s + c])
                wait("sync", stored)
                hs = c * (H // KC)
                for i, j in enumerate(K_PART):
                    m = dma(keys[i * D:(i + 1) * D, hs:hs + H // KC, s * SK:(s + 1) * SK],
                            k_parts[j, c * P:(c + 1) * P, s * SK:(s + 1) * SK].rearrange("(h d) n -> d h n", d=D),
                            s_kin[s])
            k_ready.append(m)
            for pair in range(SK // P // 2):
                i, bank = borrow()
                for j in range(2):
                    o, kt = bank[:, j * C:(j + 1) * C], pair * 2 + j
                    matmul(o, ones_row[:, :], vb_row[:, :], start=True, stop=False)
                    for k in range(KC):
                        m = matmul(o, xd[:, k, kt * P:(kt + 1) * P], vw[:, k, :], start=False,
                                   stop=(k == KC - 1), sig=s_pe)
                xd_read = m
                wait("scalar", m)
                kt = s * (SK // P) + pair * 2
                v_ready = act(values[:, kt:kt + 2, :, 0:D],
                              bank.rearrange("p (t h d) -> p t h d", t=2, h=H), None)
                give_back(i, v_ready)

        v_ready = None
        norm_slice(0)
        wait("vector", consts)
        identb_ready = dve(lambda e: e.tensor_copy(identb[:, :], ident[:, :]))
        qbs_ready = dve(lambda e: e.tensor_scalar(qbs[:, :], qb[:, :], SCALE, None, ALU.mult))
        for s in range(NSC):
            if s + 1 < NSC:
                norm_slice(s + 1)
            keys_of_slice(s)

        q_ready = {}
        q_stored = {}
        scores_mark = {}
        q_rows_ready = {}
        unit = {"n": 0, "max": []}
        tile = {"n": 0, "exp": []}
        quad_done = []
        oT_read = attn_read = None

        def queries_of(pair):
            c, hc, par, slot = pair // KC, pair % KC, pair % 2, (2 * pair) % SLOTS
            bank = borrow()
            wait("tensor", xnT_ready[-1])
            for k in range(KC):
                m = matmul(bank[1], qw[:, k, hc * P:(hc + 1) * P], xnT[:, k, 1 + c * CH:1 + (c + 1) * CH],
                           start=(k == 0), stop=(k == KC - 1), sig=s_pe)
            wait("sync", q_ready.get(pair - 2))
            wait("scalar", qbs_ready)
            stored = split(bank, m, qbs[:, hc:hc + 1], SCALE, "gpsimd", s_pool,
                           lambda j: q_parts[par, j, :, :], s_qout[par])
            wait("sync", stored, scores_mark.get(2 * pair - SLOTS + 1))
            for i, j in enumerate(Q_PART):
                m = dma(queries[i * D:(i + 1) * D, slot:slot + 2, :, :].rearrange("d b g n -> d (b g) n"),
                        q_parts[par, j, :, :].rearrange("(h d) n -> d h n", d=D), s_qin[par])
            q_ready[pair] = m

        def max_unit(b, q, g, h):
            n, head = unit["n"], b % NG * G + g
            unit["n"] += 1
            bank = wide[n % 2]
            wait("tensor", q_ready[b // 2])
            if n >= 2:
                wait("tensor", unit["max"][n - 2])
            if b == 0:
                wait("tensor", *k_ready[NSC // 2 * h:NSC // 2 * (h + 1)])
            for j in range(2):
                at = h * (NK // 2) + j * BANK
                m = matmul(bank[:, j * BANK:(j + 1) * BANK], queries[0:SPLIT, b % SLOTS, g, q * P:(q + 1) * P],
                           keys[0:SPLIT, head, at:at + BANK], sig=s_max_scores if j else None)
            wait("vector", m)
            unit["max"].append(dve(lambda e: e.tensor_reduce(maxes[:, b % 2, q, g, h:h + 1], bank[:, :],
                                                             AX_X, ALU.max), s_max))

        def max_units(b):
            if b == 0:
                return [(b, q, g, h) for h in range(2) for q in range(QT) for g in range(G)]
            return [(b, q, g, h) for q in range(QT) for g in range(G) for h in range(2)]

        mparts_read = None

        def split_max(b):
            cols = mparts[:, :, :].rearrange("p t (g w) -> p t g w", g=G)
            mx = maxes[:, b % 2, :, :, :]
            wait("vector", unit["max"][-1], mparts_read, pool_consts)
            m = dve(lambda e: e.tensor_tensor(maxs[:, :, :], mx[:, :, :, 0], mx[:, :, :, 1], ALU.max))
            left = maxs
            for j in range(PARTS):
                wait("vector", m)
                m = dve(lambda e, j=j, a=left: e.tensor_copy(cols[:, :, :, j], a[:, :, :]))
                if j < PARTS - 1:
                    wait("vector", m)
                    m = dve(lambda e, j=j, a=left: e.tensor_tensor(maxr[:, :, :], a[:, :, :], cols[:, :, :, j],
                                                                   ALU.subtract))
                    left = maxr
            return m

        def place_max(b, ready):
            nonlocal mparts_read
            i, bank = borrow()
            turned = bank[:, 0:BANK // 2].bitcast(BF16)
            wait("tensor", ready, identb_ready)
            for q in range(QT):
                m = transpose(turned[:, q * P:(q + 1) * P], mparts[:, q, :], identb[:, :], s_pe)
            mparts_read = m
            wait("scalar", m, scores_mark.get(b - SLOTS))
            for g in range(G):
                m = act(queries[SPLIT:ROWS, b % SLOTS, g, :], turned[32 * g:32 * g + PARTS, :], None)
            give_back(i, m)
            q_rows_ready[b] = m

        def score_tile(b, kt, g):
            n, head = tile["n"], b % NG * G + g
            tile["n"] += 1
            bank = score_bank[n % 2]
            if kt == 0 and g == 0:
                wait("tensor", q_rows_ready[b], minus_ones, free.get(0), free.get(1))
            if n >= 2:
                wait("tensor", tile["exp"][n - 2])
            m = matmul(bank[:, :], keys[0:ROWS, head, kt * P:(kt + 1) * P], queries[0:ROWS, b % SLOTS, g, :],
                       sig=s_scores)
            scores_mark[b] = m
            wait("scalar", m)
            if n < RING:
                wait("scalar", xs_read[0], xs_read[1])
            else:
                wait("scalar", quad_done[n // G - 2])
            tile["exp"].append(act(probs[n % RING], bank[:, :], ACT.Exp, sig=s_exp))

        def times_v(step):
            nonlocal pv_read
            b, kt = step // KT, step % KT
            wait("tensor", tile["exp"][G * step + G - 1], v_ready)
            if kt == 0:
                wait("tensor", pv_read)
            for g in range(G):
                m = matmul(pv_bank[32 * g:32 * g + VW, :], values[:, kt, b % NG * G + g, :],
                           probs[(G * step + g) % RING], start=(kt == 0), stop=(kt == KT - 1),
                           sig=s_pv if g == G - 1 else None)
            quad_done.append(m)

        def copy_sums():
            nonlocal pv_read, oT_ready
            wait("scalar", quad_done[-1], oT_read)
            oT_ready = pv_read = act(oT[:, :], pv_bank[:, :], None)

        oT_ready = None

        def divide_sums(b):
            nonlocal oT_read, attn_ready
            i, bank = borrow()
            wait("tensor", oT_ready)
            for q in range(QT):
                m = transpose(bank[:, q * P:(q + 1) * P], oT[:, q * P:(q + 1) * P], ident[:, :], s_pe)
            oT_read = m
            sums = bank.rearrange("p (t g w) -> p t g w", t=QT, g=G)
            wait("vector", m, attn_read)
            m = dve(lambda e: e.reciprocal(rden[:, :, :], sums[:, :, :, D]))
            wait("vector", m)
            at = b % NG * G * D
            attn_ready = dve(lambda e: e.tensor_tensor(
                attn[:, :, at:at + G * D].rearrange("p t (g d) -> p t g d", g=G), sums[:, :, :, 0:D],
                rden[:, :, :].unsqueeze(3).broadcast_to([P, QT, G, D]), ALU.mult))
            give_back(i, attn_ready)

        attn_ready = None

        w_ready = {}

        def ternary(w, t1, t2, ready):
            wait("gpsimd", ready)
            for issue in (lambda e: e.tensor_scalar(t1, w, wstat[:, 1:2], None, ALU.is_gt),
                          lambda e: e.tensor_scalar(t2, w, wstat[:, 2:3], None, ALU.is_lt),
                          lambda e: e.tensor_tensor(t1, t1, t2, ALU.subtract),
                          lambda e: e.tensor_tensor(t1, t1, w, ALU.subtract),
                          lambda e: e.tensor_tensor(w, w, t1, ALU.add),
                          lambda e: e.tensor_scalar(w, w, wstat[:, 0:1], None, ALU.mult)):
                m = pool(issue)
                wait("gpsimd", m)
            return m

        def scales(w, width, ready):
            wait("vector", ready, wstat_read[0])
            m = dve(lambda e: e.tensor_reduce(wstat[:, 3:4], w, AX_X, ALU.add, apply_absolute_value=True))
            wait("vector", m)
            m = dve(lambda e: e.tensor_scalar(wstat[:, 0:1], wstat[:, 3:4], 1.0 / width, SCALE_MIN,
                                              ALU.mult, ALU.max))
            wait("vector", m)
            dve(lambda e: e.tensor_scalar(wstat[:, 1:2], wstat[:, 0:1], 0.5, None, ALU.mult))
            return dve(lambda e: e.tensor_scalar(wstat[:, 2:3], wstat[:, 0:1], -0.5, None, ALU.mult))

        wstat_read = [None]

        def ffn_weights():
            i, bank = borrow()
            wait("tensor", late_consts)
            m = matmul(bank[0:R, 0:C], fbT[:, :], vlr[:, :], sig=s_pe)
            wait("vector", m, late_consts)
            low_ready = dve(lambda e: e.tensor_scalar(low[:, :], bank[0:R, 0:C], gcol[:, 0:1], None, ALU.mult))
            give_back(i, low_ready)
            yield
            tmp = [None, None]
            for f in range(FT):
                base = f % 2 * 3 * C
                w, t1, t2 = (r2[:, base + i * C:base + (i + 1) * C] for i in range(3))
                wait("sync", xd_read, tmp[f % 2])
                m = dma(w, w_fc[f * P:(f + 1) * P, :], s_w[f % 2])
                m = ternary(w, t1, t2, scales(w, C, m))
                wstat_read[0] = m
                yield
                i, bank = borrow()
                wait("tensor", m, low_ready)
                for k in range(KC):
                    o = bank[:, k * P:(k + 1) * P]
                    matmul(o, w[:, k * P:(k + 1) * P], ident[:, :], start=True, stop=False)
                    m = matmul(o, low[:, k * P:(k + 1) * P], uTs[:, f * P:(f + 1) * P], start=False, stop=True,
                               sig=s_pe)
                tmp[f % 2] = m
                wait("scalar", m, xd_read)
                w_ready[1] = act(w1[:, :, f * P:(f + 1) * P],
                                 bank[:, 0:C].rearrange("p (k n) -> p k n", k=KC), None)
                give_back(i, w_ready[1])
                yield
            wide_w = r2[:, 0:F]
            for c in range(KC):
                wait("sync", tmp[0], tmp[1])
                ready = dma(wide_w, w_proj[c * P:(c + 1) * P, :], s_w[c % 2])
                ready = scales(wide_w, F, ready)
                for h in range(2):
                    w = wide_w[:, h * BANK:(h + 1) * BANK]
                    m = ternary(w, r2[:, F:F + BANK], r2[:, F + BANK:F + 2 * BANK], ready)
                    yield
                    i, bank = borrow()
                    wait("tensor", m)
                    for j in range(4):
                        m2 = transpose(bank[:, j * P:(j + 1) * P], w[:, j * P:(j + 1) * P], ident[:, :], s_pe)
                    wait("scalar", m2)
                    w_ready[2] = act(w2[:, 4 * h:4 * h + 4, c * P:(c + 1) * P],
                                     bank.rearrange("p (j n) -> p j n", j=4), None)
                    give_back(i, w_ready[2])
                wstat_read[0] = m
                tmp = [m2, m2]
                yield
            r2_read[0] = m2

        r2_read = [None]
        state = {"stored": None, "attnT": None, "relu": None}

        def chunk_tail(c):
            nonlocal attn_read, stats_read
            rows = out[c * CH:(c + 1) * CH, :].rearrange("(t p) c -> p t c", p=P)
            wait("sync", state["stored"])
            m = dma(x1[:, :, :], x[c * CH:(c + 1) * CH, :].rearrange("(t p) c -> p t c", p=P), s_xload)
            wait("gpsimd", m, late_consts)
            x1_ready = pool(lambda e: e.tensor_tensor(
                x1[:, :, :], x1[:, :, :], ob_all[:, :].unsqueeze(1).broadcast_to([P, QT, C]), ALU.add))

            def turn(ready, k):
                i, bank = borrow()
                wait("tensor", ready)
                for q in range(QT):
                    m = transpose(bank[:, q * P:(q + 1) * P], attn[:, q, k * P:(k + 1) * P], ident[:, :], s_pe)
                wait("scalar", m, state["attnT"])
                got = act(attnT[:, k, :], bank, None)
                give_back(i, got)
                return m, got

            for k in range(KC):
                attn_read, turned = turn(attn_ready, k)
                yield
            for pair in range(QT // 2):
                i, bank = borrow()
                wait("tensor", turned, late_consts)
                for j in range(2):
                    q = 2 * pair + j
                    for k in range(KC):
                        m = matmul(bank[:, j * C:(j + 1) * C], attnT[:, k, q * P:(q + 1) * P], ow[:, k, :],
                                   start=(k == 0), stop=(k == KC - 1), sig=s_pe)
                state["attnT"] = m
                wait("vector", m, x1_ready)
                m = dve(lambda e, pair=pair, bank=bank: e.tensor_tensor(
                    x1[:, 2 * pair:2 * pair + 2, :], bank.rearrange("p (t c) -> p t c", t=2),
                    x1[:, 2 * pair:2 * pair + 2, :], ALU.add))
                give_back(i, m)
                yield
            ready = layer_norm_stats(x1, QT, m, stats_read)
            wait("gpsimd", ready, attn_read)
            for q in range(QT):
                stats_read = normalise("gpsimd", s_pool, attn, x1, q)
            normed = stats_read
            yield
            for k in range(KC):
                attn_read, turned = turn(normed, k)
                yield
            for th in range(2):
                for fp in range(FT // 2):
                    i, bank = borrow()
                    wait("tensor", turned, w_ready[1])
                    for j in range(2):
                        f = 2 * fp + j
                        for k in range(KC):
                            m = matmul(bank[:, j * C:(j + 1) * C], w1[:, k, f * P:(f + 1) * P],
                                       attnT[:, k, th * C:(th + 1) * C], start=(k == 0), stop=(k == KC - 1), sig=s_pe)
                    state["attnT"] = m
                    wait("scalar", m, state["relu"])
                    m = act(relu[:, :], bank, ACT.Relu)
                    give_back(i, m)
                    wait("gpsimd", m, r2_read[0])
                    m = pool(lambda e, fp=fp: e.tensor_tensor(r2[:, fp * BANK:(fp + 1) * BANK], relu[:, :],
                                                              relu[:, :], ALU.mult))
                    state["relu"] = m
                    hidden_ready = m
                    yield
                i, bank = borrow()
                for j in range(2):
                    wait("tensor", hidden_ready, w_ready[2])
                    for f in range(FT):
                        at = f * C + j * P
                        m = matmul(bank[:, j * C:(j + 1) * C], r2[:, at:at + P], w2[:, f, :],
                                   start=(f == 0), stop=(f == FT - 1), sig=s_pe)
                r2_read[0] = m
                wait("vector", m)
                m = dve(lambda e, th=th, bank=bank: e.tensor_tensor(
                    x1[:, 2 * th:2 * th + 2, :], bank.rearrange("p (t c) -> p t c", t=2),
                    x1[:, 2 * th:2 * th + 2, :], ALU.add))
                give_back(i, m)
                wait("sync", m)
                state["stored"] = dma(rows[:, 2 * th:2 * th + 2, :], x1[:, 2 * th:2 * th + 2, :], s_store)
                yield

        queries_of(0)
        wait("gpsimd", split_read["full"])
        minus_ones = pool(lambda e: e.memset(keys[SPLIT:ROWS, :, :].bitcast(F32), MINUS_ONES))
        wait("gpsimd", minus_ones)
        lent["banks"], lent["next"] = [3], 0
        units = [u for b in range(NB) for u in max_units(b)]
        per_step = len(max_units(0)) // KT
        taken = per_step * (KT + LEAD)
        for u in units[:per_step * KT]:
            max_unit(*u)
        parts0 = split_max(0)
        place_max(0, parts0)
        for u in units[per_step * KT:taken]:
            max_unit(*u)
        stage = ffn_weights()
        for step in range(NB * KT + 1):
            b, kt = step // KT, step % KT
            if b < NB:
                later = units[taken:taken + per_step]
                taken += per_step
                score_tile(b, kt, 0)
                score_tile(b, kt, 1)
                for u in later[:1]:
                    max_unit(*u)
                score_tile(b, kt, 2)
                for u in later[1:]:
                    max_unit(*u)
                score_tile(b, kt, 3)
                if kt == KT - LEAD - 1 and b + 1 < NB:
                    parts = split_max(b + 1)
                if kt == KT - LEAD + 1 and b + 1 < NB:
                    place_max(b + 1, parts)
                if kt == 1 and b % 2 == 0 and b + 2 < NB:
                    queries_of(b // 2 + 1)
                if kt == 2 and b > 0:
                    divide_sums(b - 1)
                if kt in (3, 5, 7, 9, 11, 15):
                    if kt == 3 and b % NG == 0 and b > 0:
                        stage = chunk_tail(b // NG - 1)
                    next(stage, None)
            if step > 0:
                times_v(step - 1)
                if step % KT == 0:
                    copy_sums()
        lent["banks"], lent["next"] = [3, 0, 1], 0
        free[0], free[1] = tile["exp"][-2], tile["exp"][-1]
        divide_sums(NB - 1)
        for _ in chunk_tail(NCH - 1):
            pass
        for s in s_kout + s_qout + [s_store]:
            wait("sync", (s["sem"], s["count"]))

        with nc.Block() as block:
            @block.tensor
            def _(e):
                issue_all("tensor", e)

            @block.vector
            def _(e):
                issue_all("vector", e)

            @block.scalar
            def _(e):
                issue_all("scalar", e)

            @block.gpsimd
            def _(e):
                issue_all("gpsimd", e)

            @block.sync
            def _(e):
                issue_all("sync", e)


def kernel(**inputs):
    import numpy as np
    import concourse.bacc as bacc
    from concourse.bass_utils import run_bass_kernel_spmd

    def get(name):
        return np.asarray(inputs[name])

    def by_partition(name):
        return get(name).reshape(-1, P).T

    x = get("L0_attn_x")
    arrays = {
        "x": x.reshape(x.shape[1:]),
        "q_wT": get("L0_attn_q_w").T, "q_b": by_partition("L0_attn_q_b"),
        "k_wT": get("L0_attn_k_w").T, "k_b": by_partition("L0_attn_k_b"),
        "v_wT": get("L0_attn_v_w").T, "v_b": get("L0_attn_v_b"),
        "conv_w": get("L0_attn_conv_w").reshape(x.shape[2], -1), "conv_b": by_partition("L0_attn_conv_b"),
        "o_wT": get("L0_attn_out_w").T, "o_b": get("L0_attn_out_b"),
        "fast_bT": get("L0_ffn_fast_b").T,
        "w_fc": get("L0_ffn_w_fc"), "w_proj": get("L0_ffn_w_proj"),
        "uT": get("L0_ffn_u").T, "v_lr": get("L0_ffn_v"), "gate": get("L0_ffn_gate").reshape(1),
        "ident_f": np.eye(P, dtype=np.float32),
    }
    arrays = {name: np.ascontiguousarray(a) for name, a in arrays.items()}
    nc = bacc.Bacc("TRN2", target_bir_lowering=False, num_devices=1)
    args = [nc.dram_tensor(name, a.shape, mybir.dt.from_np(a.dtype), kind="ExternalInput").ap()
            for name, a in arrays.items()]
    out = nc.dram_tensor("out", arrays["x"].shape, F32, kind="ExternalOutput").ap()
    build_layer(nc, *args, out)
    result = run_bass_kernel_spmd(nc, [arrays], core_ids=[0])
    return result.results[0]["out"].reshape(x.shape)
```

```python
import struct
from contextlib import ExitStack

import concourse.bass as bass
from concourse import mybir

F32 = mybir.dt.float32
BF16 = mybir.dt.bfloat16
ALU = mybir.AluOpType
ACT = mybir.ActivationFunctionType
AX_X = mybir.AxisListType.X

P = 128
BANK = 512
LN_EPS = 1e-5
SCALE_MIN = 1e-5
PARTS = 3
Q_PART = (0, 0, 0, 1, 1, 2)
K_PART = (0, 1, 2, 0, 1, 0)
MINUS_ONES = struct.unpack("<f", struct.pack("<I", 0xBF80BF80))[0]


def build_layer(nc, x, q_wT, q_b, k_wT, k_b, v_wT, v_b, conv_w, conv_b, o_wT, o_b,
                fast_bT, w_fc, w_proj, uT, v_lr, gate, ident_f, out):
    N, C = x.shape
    NK = N // 2
    D = 16
    H = C // D
    KC = C // P
    F = w_fc.shape[0]
    FT = F // P
    R = uT.shape[0]
    G = 4
    NG = H // G
    CH = BANK
    NCH = N // CH
    QT = CH // P
    NB = NCH * NG
    KT = NK // P
    SPLIT = len(Q_PART) * D
    ROWS = SPLIT + PARTS
    VW = D + 1
    SC = 1024
    NSC = N // SC
    SK = SC // 2
    ST = SC // P
    LEAD = 4
    SLOTS = 4
    RING = 2 * G
    SCALE = float(D) ** -0.5

    with ExitStack() as ctx:
        queue = {name: [] for name in ("tensor", "vector", "scalar", "gpsimd", "sync")}

        def counter(name):
            return {"sem": ctx.enter_context(nc.semaphore(name)), "count": 0}

        def do(engine, issue, sig=None, by=1):
            queue[engine].append((issue, sig, by))
            if sig is None:
                return None
            sig["count"] += by
            return sig["sem"], sig["count"]

        def wait(engine, *marks):
            for mark in marks:
                if mark is not None:
                    queue[engine].append((lambda e, m=mark: e.wait_ge(m[0], m[1]), None, 0))

        def issue_all(name, e):
            for issue, sig, by in queue[name]:
                ins = issue(e)
                if sig is not None:
                    ins.then_inc(sig["sem"], by)

        def sb(name, shape, dt=F32):
            return ctx.enter_context(nc.sbuf_tensor(name, shape, dt))

        keys = sb("keys", [ROWS, H, NK], BF16)
        queries = sb("queries", [ROWS, SLOTS, G, CH], BF16)
        xnT = sb("xnT", [P, KC, 1 + N])
        values = sb("values", [P, KT, H, VW])
        ring = sb("ring", [P, RING * CH])
        probs = [ring[:, i * CH:(i + 1) * CH] for i in range(RING)]
        qw = sb("qw", [P, KC, C])
        ow = sb("ow", [P, KC, C])
        w1 = sb("w1", [P, KC, F])
        kw, vw = w1[:, 0, 0:KC * C].rearrange("p (k c) -> p k c", k=KC), \
            w1[:, 1, 0:KC * C].rearrange("p (k c) -> p k c", k=KC)
        w2_all = sb("w2_all", [P, FT * C])
        w2 = w2_all[:, :].rearrange("p (f c) -> p f c", f=FT)
        full = sb("full", [P, CH])
        rest = sb("rest", [P, CH])
        part = sb("part", [P, PARTS, CH], BF16)
        r2 = sb("r2", [P, FT * C])
        xds = [r2[:, i * KC * SK:(i + 1) * KC * SK].rearrange("p (k n) -> p k n", k=KC) for i in range(2)]
        oT = sb("oT", [P, CH])
        attn_all = sb("attn_all", [P, 2 * QT * C])
        attn = attn_all[:, 0:QT * C].rearrange("p (t c) -> p t c", t=QT)
        attnT = attn_all[:, QT * C:2 * QT * C].rearrange("p (k n) -> p k n", k=KC)
        x1 = sb("x1", [P, QT, C])
        xs = [b.rearrange("p (t c) -> p t c", t=ST) for b in
              (ring[:, 0:ST * C], ring[:, ST * C:2 * ST * C], w2_all[:, :], attn_all[:, :])]
        relu = sb("relu", [P, BANK])
        mrows = sb("mrows", [P, CH], BF16)
        ow_parts = ow[:, :, :].bitcast(BF16)
        split_sets = ((full[:, :], rest[:, :], [part[:, j, :] for j in range(PARTS)]),
                      (oT[:, :], relu[:, :], [mrows[:, :], ow_parts[:, 0, :], ow_parts[:, 1, :]]))
        maxes = sb("maxes", [P, 2, QT, G, 2])
        maxs = sb("maxs", [P, QT, G])
        maxr = sb("maxr", [P, QT, G])
        mparts = sb("mparts", [P, QT, P], BF16)
        rden = sb("rden", [P, QT, G])
        stats = sb("stats", [P, NSC * ST, 6])
        meanvar = sb("meanvar", [P, NSC * ST, 2])
        rstd = sb("rstd", [P, NSC * ST])
        shift = sb("shift", [P, NSC * ST])
        half = sb("half", [P, NSC * ST])
        ident = sb("ident", [P, P])
        identb = sb("identb", [P, P], BF16)
        vb_all = sb("vb_all", [P, C])
        ob_all = sb("ob_all", [P, C])
        qb = sb("qb", [P, KC])
        qbs = sb("qbs", [P, KC])
        kb = sb("kb", [P, KC])
        cw = sb("cw", [P, KC, 3])
        cb = sb("cb", [P, KC])
        fbT = sb("fbT", [R, R])
        vlr = sb("vlr", [R, C])
        uTs = x1[0:R, :, :].rearrange("r t c -> r (t c)")
        gcol = sb("gcol", [R, 1])
        low = sb("low", [R, C])
        wstat = sb("wstat", [P, 4])

        psum = [ctx.enter_context(nc.psum_tensor(f"bank{i}", [P, BANK], F32)) for i in range(4, 8)]
        wide = [ctx.enter_context(nc.psum_tensor(f"wide{i}", [P, 2 * BANK], F32)) for i in range(2)]
        score_banks = [0, 1]
        pv_bank, misc_bank = psum[2], psum[3]

        k_parts = nc.dram_tensor("k_parts", [PARTS, C, NK], BF16).ap()
        q_parts = nc.dram_tensor("q_parts", [2, PARTS, P, CH], BF16).ap()

        s_const = counter("s_const")
        s_const2 = counter("s_const2")
        s_x = [counter(f"s_x{i}") for i in range(NSC)]
        s_kout = [counter(f"s_kout{i}") for i in range(2 * NSC)]
        s_kin = [counter(f"s_kin{i}") for i in range(NSC)]
        s_qout = [counter(f"s_qout{i}") for i in range(2)]
        s_qin = [counter(f"s_qin{i}") for i in range(2)]
        s_minus = counter("s_minus")
        s_ow = counter("s_ow")
        s_mrows = counter("s_mrows")
        s_xload = counter("s_xload")
        s_store = counter("s_store")
        s_w = [counter(f"s_w{i}") for i in range(2)]
        s_pool = counter("s_pool")
        s_dve = counter("s_dve")
        s_act = counter("s_act")
        s_pe = counter("s_pe")
        s_max_scores = counter("s_max_scores")
        s_max = counter("s_max")
        s_scores = counter("s_scores")
        s_exp = counter("s_exp")
        s_pv = counter("s_pv")

        def pe(issue, sig=s_pe):
            return do("tensor", issue, sig)

        def matmul(o, lhsT, rhs, start=True, stop=True, sig=None):
            return do("tensor", lambda e: e.matmul(o, lhsT, rhs, start=start, stop=stop), sig)

        def transpose(o, i, eye, sig=None):
            return do("tensor", lambda e: e.transpose(o, i, eye), sig)

        def dve(issue, sig=s_dve):
            return do("vector", issue, sig)

        def act(o, i, func, bias=0.0, scale=1.0, sig=s_act):
            if func is None:
                return do("scalar", lambda e: e.copy(o, i), sig)
            return do("scalar", lambda e: e.activation(o, i, func, bias=bias, scale=scale), sig)

        def pool(issue, sig=s_pool):
            return do("gpsimd", issue, sig)

        def dma(o, i, sig):
            return do("sync", lambda e: e.dma_start(o, i), sig, by=16)

        banks = [p[:, :] for p in psum] + [w[:, j * BANK:(j + 1) * BANK] for w in wide for j in range(2)]
        free = {}
        lent = {"banks": [0, 1, 3], "next": 0}

        def borrow():
            i = lent["banks"][lent["next"] % len(lent["banks"])]
            lent["next"] += 1
            wait("tensor", free.get(i))
            return i, banks[i]

        def give_back(i, reader):
            free[i] = reader

        def load_slice(s):
            return dma(xs[s], x[s * SC:(s + 1) * SC, :].rearrange("(t p) c -> p t c", p=P), s_x[s])

        def contraction(matrix):
            return matrix.rearrange("(k p) c -> p k c", p=P)

        x_loaded = {0: load_slice(0)}
        for dst, src in ((ident[:, :], ident_f), (cw[:, :, :], contraction(conv_w)), (cb[:, :], conv_b),
                         (kw, contraction(k_wT)), (kb[:, :], k_b),
                         (vw, contraction(v_wT)), (vb_all[:, :], v_b.rearrange("(a c) -> a c", a=1).broadcast_to([P, C])),
                         (qw[:, :, :], contraction(q_wT)), (qb[:, :], q_b)):
            consts = dma(dst, src, s_const)
        for s in range(1, NSC):
            x_loaded[s] = load_slice(s)
        for dst, src in ((ob_all[:, :], o_b.rearrange("(a c) -> a c", a=1).broadcast_to([P, C])),
                         (fbT[:, :], fast_bT), (vlr[:, :], v_lr), (uTs, uT),
                         (gcol[:, :], gate.rearrange("(a c) -> a c", a=1).broadcast_to([R, 1]))):
            late_consts = dma(dst, src, s_const2)

        pool(lambda e: e.memset(half[:, :], -0.5))
        pool(lambda e: e.memset(xnT[:, :, 0:1], 0.0))
        pool(lambda e: e.memset(mparts[:, :, :], 0.0))
        pool_consts = pool(lambda e: e.memset(values[:, :, :, D:VW], 1.0))
        wait("gpsimd", pool_consts)
        m = pool(lambda e: e.memset(keys[SPLIT:ROWS, 0, :].bitcast(F32), MINUS_ONES))
        wait("gpsimd", m)
        wait("sync", m)
        minus_ones = dma(keys[SPLIT:ROWS, 1:H, :], keys[SPLIT:ROWS, 0:1, :].broadcast_to([PARTS, H - 1, NK]),
                         s_minus)
        pv_read = dve(lambda e: e.memset(pv_bank[:, :], 0.0))

        aggregated = [None]

        def layer_norm_stats(tiles, t0, ready, stats_read):
            at = slice(t0, t0 + len(tiles))
            wait("vector", ready, aggregated[0])
            for t, tokens in enumerate(tiles):
                mark = dve(lambda e, t=t, tokens=tokens: e.bn_stats(stats[:, t0 + t, :], tokens))
            wait("vector", mark, *stats_read)
            for t in range(t0, t0 + len(tiles)):
                mark = dve(lambda e, t=t: e.bn_aggr(meanvar[:, t, :], stats[:, t, :]))
            aggregated[0] = mark
            wait("gpsimd", mark, pool_consts, *stats_read)
            mark = pool(lambda e: e.tensor_scalar(rstd[:, at], meanvar[:, at, 1], LN_EPS, None, ALU.add))
            wait("gpsimd", mark)
            mark = pool(lambda e: e.tensor_tensor(rstd[:, at], rstd[:, at], half[:, at], ALU.pow))
            wait("gpsimd", mark)
            mark = pool(lambda e: e.tensor_tensor(shift[:, at], meanvar[:, at, 0], rstd[:, at], ALU.mult))
            wait("gpsimd", mark)
            return pool(lambda e: e.tensor_scalar(shift[:, at], shift[:, at], -1.0, None, ALU.mult))

        def normalise(engine, sig, dst, src, t):
            return do(engine, lambda e: e.tensor_scalar(dst, src, rstd[:, t:t + 1], shift[:, t:t + 1],
                                                        ALU.mult, ALU.add), sig)

        split_read = [{"full": None, "parts": None} for _ in split_sets]

        def split(which, bank, ready, bias, scale, engine, sig, store, store_sig, copier=None):
            copier, copier_sig = copier or (engine, sig)

            def rounding(dst, src):
                if copier == "scalar":
                    return lambda e: e.copy(dst, src)
                if copier == "gpsimd":
                    return lambda e: e.tensor_scalar(dst, src, 1.0, 1.0, ALU.mult, ALU.mult)
                return lambda e: e.tensor_copy(dst, src)

            i, b = bank
            whole_t, rest_t, parts = split_sets[which]
            read = split_read[which]
            wait("scalar", ready, read["full"])
            whole = act(whole_t, b, ACT.Identity, bias=bias, scale=scale)
            give_back(i, whole)
            wait(copier, whole, read["parts"])
            first = do(copier, rounding(parts[0], whole_t), copier_sig)
            wait(engine, first)
            m = do(engine, lambda e: e.tensor_tensor(rest_t, whole_t, parts[0], ALU.subtract), sig)
            wait(copier, m)
            second = do(copier, rounding(parts[1], rest_t), copier_sig)
            wait(engine, second)
            third = do(engine, lambda e: e.tensor_tensor(parts[2], rest_t, parts[1], ALU.subtract), sig)
            for j, mark in enumerate((first, second, third)):
                wait("sync", mark)
                stored = dma(store(j), parts[j], store_sig)
            read["full"], read["parts"] = third, stored
            return stored

        norm_ready = {}
        normalised = []
        xs_read = [None] * NSC
        xd_read, xd_ready = [None, None], [None, None]
        xnT_ready, k_ready = [], []

        def stats_of_slice(s):
            norm_ready[s] = layer_norm_stats([xs[s][:, t, :] for t in range(ST)], s * ST, x_loaded[s], ())

        def turn_slice(s):
            wait("scalar", norm_ready[s])
            wait("gpsimd", norm_ready[s])
            for t in range(ST):
                tokens, col = xs[s][:, t, :], s * ST + t
                if t % 2:
                    mark = act(tokens, tokens, ACT.Identity, bias=shift[:, col:col + 1], scale=rstd[:, col:col + 1])
                else:
                    even = normalise("gpsimd", s_pool, tokens, tokens, col)
                    wait("tensor", even)
                if t % QT == QT - 1:
                    wait("tensor", mark, consts)
                    for k in range(KC):
                        i, bank = borrow()
                        for j in range(QT):
                            m = transpose(bank[:, j * P:(j + 1) * P],
                                          xs[s][:, t - QT + 1 + j, k * P:(k + 1) * P], ident[:, :], s_pe)
                        wait("scalar", m)
                        at = 1 + s * SC + (t // QT) * BANK
                        got = act(xnT[:, k, at:at + BANK], bank, None)
                        give_back(i, got)
                    xs_read[s] = m
            normalised.extend((mark, even))
            xnT_ready.append(got)

        v_ready = None

        def convolve(s):
            xd = xds[s % 2]
            wait("vector", xnT_ready[s], xd_read[s % 2], consts, pool_consts)
            for k in range(KC):
                tap = [xnT[:, k, s * SC + i:s * SC + i + 2 * SK - 1:2] for i in range(3)]
                m = dve(lambda e, k=k, a=tap[1]: e.tensor_scalar(xd[:, k, :], a, cw[:, k, 1:2], cb[:, k:k + 1],
                                                                 ALU.mult, ALU.add))
                for i in (0, 2):
                    wait("vector", m)
                    m = dve(lambda e, k=k, i=i, a=tap[i]: e.scalar_tensor_tensor(
                        out=xd[:, k, :], in0=a, scalar=cw[:, k, i:i + 1], in1=xd[:, k, :],
                        op0=ALU.mult, op1=ALU.add))
            xd_ready[s % 2] = m

        def keys_of_slice(s):
            xd = xds[s % 2]
            wait("tensor", xd_ready[s % 2])
            for c in range(KC):
                bank = borrow()
                for k in range(KC):
                    m = matmul(bank[1], kw[:, k, c * P:(c + 1) * P], xd[:, k, :], start=(k == 0),
                               stop=(k == KC - 1), sig=s_pe)
                engine, sig = (("vector", s_dve), ("gpsimd", s_pool))[c]
                stored = split(c, bank, m, kb[:, c:c + 1], 1.0, engine, sig,
                               lambda j, c=c: k_parts[j, c * P:(c + 1) * P, s * SK:(s + 1) * SK], s_kout[2 * s + c],
                               copier=("scalar", s_act) if c else None)
                wait("sync", stored)
                hs = c * (H // KC)
                for i, j in enumerate(K_PART):
                    m = dma(keys[i * D:(i + 1) * D, hs:hs + H // KC, s * SK:(s + 1) * SK],
                            k_parts[j, c * P:(c + 1) * P, s * SK:(s + 1) * SK].rearrange("(h d) n -> d h n", d=D),
                            s_kin[s])
            k_ready.append(m)

        def values_of_slice(s):
            nonlocal v_ready
            xd = xds[s % 2]
            for pair in range(SK // P // 2):
                i, bank = borrow()
                for j in range(2):
                    o, kt = bank[:, j * C:(j + 1) * C], pair * 2 + j
                    for k in range(KC):
                        m = matmul(o, xd[:, k, kt * P:(kt + 1) * P], vw[:, k, :], start=(k == 0),
                                   stop=(k == KC - 1), sig=s_pe)
                xd_read[s % 2] = m
                wait("vector", m)
                kt = s * (SK // P) + pair * 2
                v_ready = dve(lambda e, kt=kt, bank=bank: e.tensor_tensor(
                    values[:, kt:kt + 2, :, 0:D], bank.rearrange("p (t h d) -> p t h d", t=2, h=H),
                    vb_all[:, :].rearrange("p (h d) -> p h d", d=D).unsqueeze(1).broadcast_to([P, 2, H, D]), ALU.add))
                give_back(i, v_ready)

        q_ready = {}
        q_stored = {}
        scores_mark = {}
        q_rows_ready = {}
        unit = {"n": 0, "max": []}
        tile = {"n": 0, "exp": []}
        quad_done = []
        oT_read = attn_read = relu_read = mrows_read = None

        def queries_of(pair, engine="gpsimd", sig=s_pool, copier=None):
            c, hc, par, slot = pair // KC, pair % KC, pair % 2, (2 * pair) % SLOTS
            bank = borrow()
            wait("tensor", xnT_ready[c * CH // SC])
            for k in range(KC):
                m = matmul(bank[1], qw[:, k, hc * P:(hc + 1) * P], xnT[:, k, 1 + c * CH:1 + (c + 1) * CH],
                           start=(k == 0), stop=(k == KC - 1), sig=s_pe)
            wait("sync", q_ready.get(pair - 2))
            wait("scalar", qbs_ready)
            stored = split(0, bank, m, qbs[:, hc:hc + 1], SCALE, engine, sig,
                           lambda j: q_parts[par, j, :, :], s_qout[par], copier)
            wait("sync", stored, scores_mark.get(2 * pair - SLOTS + 1))
            for i, j in enumerate(Q_PART):
                m = dma(queries[i * D:(i + 1) * D, slot:slot + 2, :, :].rearrange("d b g n -> d (b g) n"),
                        q_parts[par, j, :, :].rearrange("(h d) n -> d h n", d=D), s_qin[par])
            q_ready[pair] = m

        def max_scores(b, q, g, h, j):
            n, head = unit["n"], b % NG * G + g
            bank = wide[n % 2]
            if j == 0:
                wait("tensor", q_ready[b // 2])
                if n >= 2:
                    wait("tensor", unit["max"][n - 2])
                if b == 0:
                    wait("tensor", *k_ready[NSC // 2 * h:NSC // 2 * (h + 1)])
            at = h * (NK // 2) + j * BANK
            m = matmul(bank[:, j * BANK:(j + 1) * BANK], queries[0:SPLIT, b % SLOTS, g, q * P:(q + 1) * P],
                       keys[0:SPLIT, head, at:at + BANK], sig=s_max_scores if j else None)
            if j == 1:
                unit["n"] += 1
                wait("vector", m, maxes_read[b % 2])
                unit["max"].append(dve(lambda e: e.tensor_reduce(maxes[:, b % 2, q, g, h:h + 1], bank[:, :],
                                                                 AX_X, ALU.max), s_max))

        oT_ready = attn_ready = None

        def max_units(b):
            if b == 0:
                return [(b, q, g, h, j) for h in range(2) for q in range(QT) for g in range(G) for j in range(2)]
            return [(b, q, g, h, j) for q in range(QT) for g in range(G) for h in range(2) for j in range(2)]

        mparts_read = None
        maxes_read = [None, None]
        maxs_read = None

        def split_max(b):
            nonlocal maxs_read
            cols = mparts[:, :, :].rearrange("p t (g w) -> p t g w", g=G)
            mx = maxes[:, b % 2, :, :, :]
            wait("vector", unit["max"][-1], maxs_read)
            maxes_read[b % 2] = m = dve(lambda e: e.tensor_tensor(maxs[:, :, :], mx[:, :, :, 0], mx[:, :, :, 1],
                                                                  ALU.max))
            wait("gpsimd", mparts_read)
            left = maxs
            for j in range(PARTS):
                wait("gpsimd", m)
                m = pool(lambda e, j=j, a=left: e.tensor_scalar(cols[:, :, :, j], a[:, :, :], 1.0, 1.0,
                                                                ALU.mult, ALU.mult))
                if j < PARTS - 1:
                    wait("gpsimd", m)
                    m = pool(lambda e, j=j, a=left: e.tensor_tensor(maxr[:, :, :], a[:, :, :], cols[:, :, :, j],
                                                                    ALU.subtract))
                    left = maxr
            maxs_read = m
            return m

        def place_max(b, ready):
            nonlocal mparts_read
            i, bank = borrow()
            turned = bank[:, 0:BANK // 2].bitcast(BF16)
            wait("tensor", ready, identb_ready)
            for q in range(QT):
                m = transpose(turned[:, q * P:(q + 1) * P], mparts[:, q, :], identb[:, :], s_pe)
            mparts_read = m
            wait("scalar", m, q_rows_ready.get(b - 1, mrows_read))
            m = act(mrows[:, :], turned, None)
            give_back(i, m)
            wait("sync", m, scores_mark.get(b - SLOTS))
            for g in range(G):
                m = dma(queries[SPLIT:ROWS, b % SLOTS, g, :], mrows[32 * g:32 * g + PARTS, :], s_mrows)
            q_rows_ready[b] = m

        def score_tile(b, kt, g):
            n, head = tile["n"], b % NG * G + g
            tile["n"] += 1
            in_use = score_banks if b < NB - 1 else score_banks + [4, 5, 6, 7]
            i = in_use[n % len(in_use)]
            bank = banks[i]
            if kt == 0 and g == 0:
                wait("tensor", q_rows_ready[b], minus_ones)
            wait("tensor", free.get(i))
            m = matmul(bank, keys[0:ROWS, head, kt * P:(kt + 1) * P], queries[0:ROWS, b % SLOTS, g, :],
                       sig=s_scores)
            scores_mark[b] = m
            wait("scalar", m)
            if n < RING:
                wait("scalar", xs_read[n * CH // (ST * C)])
            else:
                wait("scalar", quad_done[n // G - 2])
            tile["exp"].append(act(probs[n % RING], bank, ACT.Exp, sig=s_exp))
            free[i] = tile["exp"][-1]

        def times_v(step):
            nonlocal pv_read
            b, kt = step // KT, step % KT
            wait("tensor", tile["exp"][G * step + G - 1], v_ready)
            if kt == 0:
                wait("tensor", pv_read)
            for g in range(G):
                m = matmul(pv_bank[32 * g:32 * g + VW, :], values[:, kt, b % NG * G + g, :],
                           probs[(G * step + g) % RING], start=(kt == 0), stop=(kt == KT - 1),
                           sig=s_pv if g == G - 1 else None)
            quad_done.append(m)

        def copy_sums():
            nonlocal pv_read, oT_ready
            wait("scalar", quad_done[-1], oT_read)
            oT_ready = pv_read = act(oT[:, :], pv_bank[:, :], None)

        def divide_sums(b):
            nonlocal oT_read, attn_ready
            i, bank = borrow()
            wait("tensor", oT_ready)
            for q in range(QT):
                m = transpose(bank[:, q * P:(q + 1) * P], oT[:, q * P:(q + 1) * P], ident[:, :], s_pe)
            oT_read = m
            sums = bank.rearrange("p (t g w) -> p t g w", t=QT, g=G)
            wait("vector", m, attn_read)
            m = dve(lambda e: e.reciprocal(rden[:, :, :], sums[:, :, :, D]))
            wait("vector", m)
            at = b % NG * G * D
            attn_ready = dve(lambda e: e.tensor_tensor(
                attn[:, :, at:at + G * D].rearrange("p t (g d) -> p t g d", g=G), sums[:, :, :, 0:D],
                rden[:, :, :].unsqueeze(3).broadcast_to([P, QT, G, D]), ALU.mult))
            give_back(i, attn_ready)

        w_ready = {}

        def ternary(w, t1, t2, ready):
            wait("gpsimd", ready)
            for issue in (lambda e: e.tensor_scalar(t1, w, wstat[:, 1:2], None, ALU.is_gt),
                          lambda e: e.tensor_scalar(t2, w, wstat[:, 2:3], None, ALU.is_lt),
                          lambda e: e.tensor_tensor(t1, t1, t2, ALU.subtract),
                          lambda e: e.tensor_tensor(t1, t1, w, ALU.subtract),
                          lambda e: e.tensor_tensor(w, w, t1, ALU.add),
                          lambda e: e.tensor_scalar(w, w, wstat[:, 0:1], None, ALU.mult)):
                m = pool(issue)
                wait("gpsimd", m)
            return m

        def scales(w, width, ready):
            wait("vector", ready, wstat_read[0])
            m = dve(lambda e: e.tensor_reduce(wstat[:, 3:4], w, AX_X, ALU.add, apply_absolute_value=True))
            wait("vector", m)
            m = dve(lambda e: e.tensor_scalar(wstat[:, 0:1], wstat[:, 3:4], 1.0 / width, SCALE_MIN,
                                              ALU.mult, ALU.max))
            wait("vector", m)
            dve(lambda e: e.tensor_scalar(wstat[:, 1:2], wstat[:, 0:1], 0.5, None, ALU.mult))
            return dve(lambda e: e.tensor_scalar(wstat[:, 2:3], wstat[:, 0:1], -0.5, None, ALU.mult))

        wstat_read = [None]

        def ffn_weights():
            i, bank = borrow()
            wait("tensor", late_consts)
            m = matmul(bank[0:R, 0:C], fbT[:, :], vlr[:, :], sig=s_pe)
            wait("vector", m, late_consts)
            low_ready = dve(lambda e: e.tensor_scalar(low[:, :], bank[0:R, 0:C], gcol[:, 0:1], None, ALU.mult))
            give_back(i, low_ready)
            yield
            tmp = [None, None]

            def hidden_rows(f):
                base = f % 2 * 3 * C
                w, t1, t2 = (r2[:, base + i * C:base + (i + 1) * C] for i in range(3))
                wait("sync", xd_read[0], xd_read[1], tmp[f % 2])
                m = dma(w, w_fc[f * P:(f + 1) * P, :], s_w[f % 2])
                wstat_read[0] = ternary(w, t1, t2, scales(w, C, m))
                return w, wstat_read[0]

            following = hidden_rows(0)
            yield
            for f in range(FT):
                (w, m), following = following, hidden_rows(f + 1) if f + 1 < FT else None
                i, bank = borrow()
                wait("tensor", m, low_ready)
                for k in range(KC):
                    o = bank[:, k * P:(k + 1) * P]
                    matmul(o, w[:, k * P:(k + 1) * P], ident[:, :], start=True, stop=False)
                    m = matmul(o, low[:, k * P:(k + 1) * P], uTs[:, f * P:(f + 1) * P], start=False, stop=True,
                               sig=s_pe)
                tmp[f % 2] = m
                wait("scalar", m, xd_read[1])
                w_ready[1] = act(w1[:, :, f * P:(f + 1) * P],
                                 bank[:, 0:C].rearrange("p (k n) -> p k n", k=KC), None)
                give_back(i, w_ready[1])
                yield
            wide_w = r2[:, 0:F]
            for c in range(KC):
                wait("sync", tmp[0], tmp[1])
                ready = dma(wide_w, w_proj[c * P:(c + 1) * P, :], s_w[c % 2])
                ready = scales(wide_w, F, ready)
                for h in range(2):
                    w = wide_w[:, h * BANK:(h + 1) * BANK]
                    m = ternary(w, r2[:, F:F + BANK], r2[:, F + BANK:F + 2 * BANK], ready)
                    yield
                    yield
                    yield
                    i, bank = borrow()
                    wait("tensor", m)
                    for j in range(4):
                        m2 = transpose(bank[:, j * P:(j + 1) * P], w[:, j * P:(j + 1) * P], ident[:, :], s_pe)
                    wait("scalar", m2)
                    w_ready[2] = act(w2[:, 4 * h:4 * h + 4, c * P:(c + 1) * P],
                                     bank.rearrange("p (j n) -> p j n", j=4), None)
                    give_back(i, w_ready[2])
                wstat_read[0] = m
                tmp = [m2, m2]
                yield
            r2_read[0] = m2

        r2_read = [None]
        state = {"stored": None, "attnT": None, "relu": None}

        def chunk_tail(c):
            nonlocal attn_read, stats_read, relu_read
            last = c == NCH - 1
            HT = QT // 2
            HN = HT * P
            elementwise, ew_sig = ("vector", s_dve) if last else ("gpsimd", s_pool)
            x2 = (ring if last else r2)[:, 0:QT * C].rearrange("p (t c) -> p t c", t=QT)
            hidden = [r2[:, :], ring[:, FT * HN:2 * FT * HN] if last else r2[:, :]]
            rows = out[c * CH:(c + 1) * CH, :].rearrange("(t p) c -> p t c", p=P)
            wait("sync", state["stored"] if c else w_ready[1])
            m = dma(x1[:, :, :], x[c * CH:(c + 1) * CH, :].rearrange("(t p) c -> p t c", p=P), s_xload)
            wait("gpsimd", m, late_consts)
            x1_ready = pool(lambda e: e.tensor_tensor(
                x1[:, :, :], x1[:, :, :], ob_all[:, :].unsqueeze(1).broadcast_to([P, QT, C]), ALU.add))

            def turn(src, ready, h):
                i, bank = borrow()
                wait("tensor", ready)
                for k in range(KC):
                    for q in range(HT):
                        at = k * HN + q * P
                        m = transpose(bank[:, at:at + P], src[:, h * HT + q, k * P:(k + 1) * P], ident[:, :], s_pe)
                wait("scalar", m, state["attnT"])
                got = act(attnT[:, :, h * HN:(h + 1) * HN], bank.rearrange("p (k n) -> p k n", k=KC), None)
                give_back(i, got)
                return m, got

            turned = [None, None]
            normed = [None, None]
            for h in range(2):
                attn_read, turned[h] = turn(attn, attn_ready, h)
                yield
            for h in range(2):
                i, bank = borrow()
                wait("tensor", turned[h], ow_ready)
                for j in range(HT):
                    q = HT * h + j
                    for k in range(KC):
                        m = matmul(bank[:, j * C:(j + 1) * C], attnT[:, k, q * P:(q + 1) * P], ow[:, k, :],
                                   start=(k == 0), stop=(k == KC - 1), sig=s_pe)
                state["attnT"] = m
                tiles = x1[:, HT * h:HT * (h + 1), :]
                wait("vector", m, x1_ready)
                m = dve(lambda e, tiles=tiles, bank=bank: e.tensor_tensor(
                    tiles, bank.rearrange("p (t c) -> p t c", t=HT), tiles, ALU.add))
                give_back(i, m)
                ready = layer_norm_stats([x1[:, q, :] for q in range(HT * h, HT * (h + 1))], HT * h, m, stats_read)
                wait(elementwise, ready, r2_read[0], quad_done[-1] if last else None)
                for q in range(HT * h, HT * (h + 1)):
                    normed[h] = normalise(elementwise, ew_sig, x2[:, q, :], x1[:, q, :], q)
                stats_read = (normed[h],)
                yield
            yield
            for h in range(2):
                _, turned[h] = turn(x2, normed[h], h)
                yield

            hidden_ready = [None, None]

            def widen(h):
                nonlocal relu_read
                for fp in range(FT // 2):
                    i, bank = borrow()
                    wait("tensor", turned[h], w_ready[1])
                    for j in range(2):
                        f = 2 * fp + j
                        for k in range(KC):
                            m = matmul(bank[:, j * HN:(j + 1) * HN], w1[:, k, f * P:(f + 1) * P],
                                       attnT[:, k, h * HN:(h + 1) * HN], start=(k == 0), stop=(k == KC - 1),
                                       sig=s_pe)
                    state["attnT"] = m
                    wait("scalar", m, relu_read)
                    m = act(relu[:, :], bank, ACT.Relu)
                    give_back(i, m)
                    wait(elementwise, m, r2_read[0])
                    dst = hidden[h][:, fp * BANK:(fp + 1) * BANK]
                    relu_read = hidden_ready[h] = do(
                        elementwise, lambda e, dst=dst: e.tensor_tensor(dst, relu[:, :], relu[:, :], ALU.mult), ew_sig)
                    yield

            def narrow(h):
                i, bank = borrow()
                wait("tensor", hidden_ready[h], w_ready[2])
                for j in range(HT):
                    for f in range(FT):
                        at = f * HN + j * P
                        m = matmul(bank[:, j * C:(j + 1) * C], hidden[h][:, at:at + P], w2[:, f, :],
                                   start=(f == 0), stop=(f == FT - 1), sig=s_pe)
                r2_read[0] = m
                tiles = x1[:, HT * h:HT * (h + 1), :]
                wait("vector", m)
                m = dve(lambda e, tiles=tiles, bank=bank: e.tensor_tensor(
                    tiles, bank.rearrange("p (t c) -> p t c", t=HT), tiles, ALU.add))
                give_back(i, m)
                wait("sync", m)
                state["stored"] = dma(rows[:, HT * h:HT * (h + 1), :], tiles, s_store)

            if last:
                yield from widen(0)
                yield from widen(1)
                narrow(0)
                narrow(1)
            else:
                for h in range(2):
                    yield from widen(h)
                    narrow(h)
                    yield

        units = [u for b in range(NB) for u in max_units(b)]
        per_step = len(max_units(0)) // KT
        stats_of_slice(0)
        wait("vector", consts)
        identb_ready = dve(lambda e: e.tensor_copy(identb[:, :], ident[:, :]))
        qbs_ready = dve(lambda e: e.tensor_scalar(qbs[:, :], qb[:, :], SCALE, None, ALU.mult))
        early = 0
        early = 0

        def early_maxima(share):
            nonlocal early
            for u in units[early:early + share]:
                max_scores(*u)
            early += share

        turn_slice(0)
        stats_of_slice(1)
        convolve(0)
        turn_slice(1)
        stats_of_slice(2)
        keys_of_slice(0)
        queries_of(0, "vector", s_dve, ("scalar", s_act))
        convolve(1)
        values_of_slice(0)
        turn_slice(2)
        stats_of_slice(3)
        keys_of_slice(1)
        convolve(2)
        values_of_slice(1)
        turn_slice(3)
        keys_of_slice(2)
        convolve(3)
        early_maxima(per_step * KT // 4)
        values_of_slice(2)
        keys_of_slice(3)
        early_maxima(per_step * KT // 4)
        values_of_slice(3)
        stats_read = normalised
        lent["banks"], lent["next"] = [3], 0
        wait("sync", split_read[1]["full"], split_read[1]["parts"])
        ow_ready = dma(ow[:, :, :], contraction(o_wT), s_ow)
        oT_read, relu_read, mrows_read = (split_read[1]["full"],) * 2 + (split_read[1]["parts"],)
        taken = per_step * KT
        early_maxima(taken - early)
        parts0 = split_max(0)
        early_maxima(2 * per_step)
        place_max(0, parts0)
        early_maxima(per_step)
        taken = early
        stage = ffn_weights()
        for step in range(NB * KT + 1):
            b, kt = step // KT, step % KT
            if step == (NB - 1) * KT:
                free.update({i: unit["max"][-1] for i in range(4, 8)})
            if b < NB:
                target = min(per_step * (step + 1 + KT + LEAD),
                             early + -(-(2 * per_step * KT - early) * (step + 1) // (KT - LEAD)))
                later = units[taken:target]
                taken = target
                score_tile(b, kt, 0)
                score_tile(b, kt, 1)
                for u in later[:3]:
                    max_scores(*u)
                score_tile(b, kt, 2)
                for u in later[3:]:
                    max_scores(*u)
                score_tile(b, kt, 3)
                if kt == KT - LEAD - 1 and b + 1 < NB:
                    parts = split_max(b + 1)
                if kt == KT - LEAD + 1 and b + 1 < NB:
                    place_max(b + 1, parts)
                if kt == 1 and b % 2 == 0 and b + 2 < NB:
                    queries_of(b // 2 + 1)
                if kt == 2 and b > 0:
                    divide_sums(b - 1)
                if kt in (3, 5, 7, 9, 11, 15):
                    if kt == 3 and b % NG == 0 and b > 0:
                        for _ in stage:
                            pass
                        stage = chunk_tail(b // NG - 1)
                    next(stage, None)
            if step > 0:
                times_v(step - 1)
                if step % KT == 0:
                    copy_sums()
        lent["banks"], lent["next"] = [3, 0, 1, 4, 5, 6, 7], 0
        divide_sums(NB - 1)
        for _ in chunk_tail(NCH - 1):
            pass
        for s in s_kout + s_qout + [s_store]:
            wait("sync", (s["sem"], s["count"]))

        with nc.Block() as block:
            @block.tensor
            def _(e):
                issue_all("tensor", e)

            @block.vector
            def _(e):
                issue_all("vector", e)

            @block.scalar
            def _(e):
                issue_all("scalar", e)

            @block.gpsimd
            def _(e):
                issue_all("gpsimd", e)

            @block.sync
            def _(e):
                issue_all("sync", e)


def kernel(**inputs):
    import numpy as np
    import concourse.bacc as bacc
    from concourse.bass_utils import run_bass_kernel_spmd

    def get(name):
        return np.asarray(inputs[name])

    def by_partition(name):
        return get(name).reshape(-1, P).T

    x = get("L0_attn_x")
    arrays = {
        "x": x.reshape(x.shape[1:]),
        "q_wT": get("L0_attn_q_w").T, "q_b": by_partition("L0_attn_q_b"),
        "k_wT": get("L0_attn_k_w").T, "k_b": by_partition("L0_attn_k_b"),
        "v_wT": get("L0_attn_v_w").T, "v_b": get("L0_attn_v_b"),
        "conv_w": get("L0_attn_conv_w").reshape(x.shape[2], -1), "conv_b": by_partition("L0_attn_conv_b"),
        "o_wT": get("L0_attn_out_w").T, "o_b": get("L0_attn_out_b"),
        "fast_bT": get("L0_ffn_fast_b").T,
        "w_fc": get("L0_ffn_w_fc"), "w_proj": get("L0_ffn_w_proj"),
        "uT": get("L0_ffn_u").T, "v_lr": get("L0_ffn_v"), "gate": get("L0_ffn_gate").reshape(1),
        "ident_f": np.eye(P, dtype=np.float32),
    }
    arrays = {name: np.ascontiguousarray(a) for name, a in arrays.items()}
    nc = bacc.Bacc("TRN2", target_bir_lowering=False, num_devices=1)
    args = [nc.dram_tensor(name, a.shape, mybir.dt.from_np(a.dtype), kind="ExternalInput").ap()
            for name, a in arrays.items()]
    out = nc.dram_tensor("out", arrays["x"].shape, F32, kind="ExternalOutput").ap()
    build_layer(nc, *args, out)
    result = run_bass_kernel_spmd(nc, [arrays], core_ids=[0])
    return result.results[0]["out"].reshape(x.shape)
```

```python
import struct
from contextlib import ExitStack

import concourse.bass as bass
from concourse import mybir

F32 = mybir.dt.float32
BF16 = mybir.dt.bfloat16
ALU = mybir.AluOpType
ACT = mybir.ActivationFunctionType
AX_X = mybir.AxisListType.X

P = 128
BANK = 512
LN_EPS = 1e-5
SCALE_MIN = 1e-5
PARTS = 3
Q_PART = (0, 0, 0, 1, 1, 2)
K_PART = (0, 1, 2, 0, 1, 0)
MINUS_ONES = struct.unpack("<f", struct.pack("<I", 0xBF80BF80))[0]


def build_layer(nc, x, q_wT, q_b, k_wT, k_b, v_wT, v_b, conv_w, conv_b, o_wT, o_b,
                fast_bT, w_fc, w_proj, uT, v_lr, gate, ident_f, out):
    N, C = x.shape
    NK = N // 2
    D = 16
    H = C // D
    KC = C // P
    F = w_fc.shape[0]
    FT = F // P
    R = uT.shape[0]
    G = 4
    NG = H // G
    CH = BANK
    NCH = N // CH
    QT = CH // P
    NB = NCH * NG
    KT = NK // P
    SPLIT = len(Q_PART) * D
    ROWS = SPLIT + PARTS
    VW = D + 1
    SC = 1024
    NSC = N // SC
    SK = SC // 2
    ST = SC // P
    LEAD = 4
    SLOTS = 4
    RING = 2 * G
    SCALE = float(D) ** -0.5

    with ExitStack() as ctx:
        queue = {name: [] for name in ("tensor", "vector", "scalar", "gpsimd", "sync")}

        def counter(name):
            return {"sem": ctx.enter_context(nc.semaphore(name)), "count": 0}

        def do(engine, issue, sig=None, by=1):
            queue[engine].append((issue, sig, by))
            if sig is None:
                return None
            sig["count"] += by
            return sig["sem"], sig["count"]

        def wait(engine, *marks):
            for mark in marks:
                if mark is not None:
                    queue[engine].append((lambda e, m=mark: e.wait_ge(m[0], m[1]), None, 0))

        def issue_all(name, e):
            for issue, sig, by in queue[name]:
                ins = issue(e)
                if sig is not None:
                    ins.then_inc(sig["sem"], by)

        def sb(name, shape, dt=F32):
            return ctx.enter_context(nc.sbuf_tensor(name, shape, dt))

        keys = sb("keys", [ROWS, H, NK], BF16)
        queries = sb("queries", [ROWS, SLOTS, G, CH], BF16)
        xnT = sb("xnT", [P, KC, 1 + N])
        values = sb("values", [P, KT, H, VW])
        ring = sb("ring", [P, RING * CH])
        probs = [ring[:, i * CH:(i + 1) * CH] for i in range(RING)]
        qw = sb("qw", [P, KC, C])
        ow = sb("ow", [P, KC, C])
        w1 = sb("w1", [P, KC, F])
        kw, vw = w1[:, 0, 0:KC * C].rearrange("p (k c) -> p k c", k=KC), \
            w1[:, 1, 0:KC * C].rearrange("p (k c) -> p k c", k=KC)
        w2_all = sb("w2_all", [P, FT * C])
        w2 = w2_all[:, :].bitcast(BF16)[:, 0:FT * C].rearrange("p (f c) -> p f c", f=FT)
        w2_scale = sb("w2_scale", [P, C])
        full = sb("full", [P, CH])
        rest = sb("rest", [P, CH])
        part = sb("part", [P, PARTS, CH], BF16)
        r2 = sb("r2", [P, FT * C])
        xds = [r2[:, i * KC * SK:(i + 1) * KC * SK].rearrange("p (k n) -> p k n", k=KC) for i in range(2)]
        oT = sb("oT", [P, CH])
        attn_all = sb("attn_all", [P, 2 * QT * C])
        attn = attn_all[:, 0:QT * C].rearrange("p (t c) -> p t c", t=QT)
        attnT = attn_all[:, QT * C:2 * QT * C].rearrange("p (k n) -> p k n", k=KC)
        x1 = sb("x1", [P, QT, C])
        xs = [b.rearrange("p (t c) -> p t c", t=ST) for b in
              (ring[:, 0:ST * C], ring[:, ST * C:2 * ST * C], w2_all[:, :], attn_all[:, :])]
        relu = sb("relu", [P, BANK])
        mrows = sb("mrows", [P, CH], BF16)
        ow_parts = ow[:, :, :].bitcast(BF16)
        split_sets = ((full[:, :], rest[:, :], [part[:, j, :] for j in range(PARTS)]),
                      (oT[:, :], relu[:, :], [mrows[:, :], ow_parts[:, 0, :], ow_parts[:, 1, :]]))
        maxes = sb("maxes", [P, 2, QT, G, 2])
        slice_maxes = sb("slice_maxes", [P, QT, G, NSC])
        maxs = sb("maxs", [P, QT, G])
        maxr = sb("maxr", [P, QT, G])
        mparts = sb("mparts", [P, QT, P], BF16)
        rden = sb("rden", [P, QT, G])
        stats = sb("stats", [P, NSC * ST, 6])
        meanvar = sb("meanvar", [P, NSC * ST, 2])
        rstd = sb("rstd", [P, NSC * ST])
        shift = sb("shift", [P, NSC * ST])
        half = sb("half", [P, NSC * ST])
        ident = sb("ident", [P, P])
        identb = sb("identb", [P, P], BF16)
        vb_all = sb("vb_all", [P, C])
        ob_all = sb("ob_all", [P, C])
        qb = sb("qb", [P, KC])
        qbs = sb("qbs", [P, KC])
        kb = sb("kb", [P, KC])
        cw = sb("cw", [P, KC, 3])
        cb = sb("cb", [P, KC])
        fbT = sb("fbT", [R, R])
        vlr = sb("vlr", [R, C])
        uTs = x1[0:R, :, :].rearrange("r t c -> r (t c)")
        gcol = sb("gcol", [R, 1])
        low = sb("low", [R, C])
        wstats = sb("wstats", [P, 3, 4])

        psum = [ctx.enter_context(nc.psum_tensor(f"bank{i}", [P, BANK], F32)) for i in range(4, 8)]
        wide = [ctx.enter_context(nc.psum_tensor(f"wide{i}", [P, 2 * BANK], F32)) for i in range(2)]
        score_banks = [0, 1]
        pv_bank, misc_bank = psum[2], psum[3]

        k_parts = nc.dram_tensor("k_parts", [PARTS, C, NK], BF16).ap()
        q_parts = nc.dram_tensor("q_parts", [2, PARTS, P, CH], BF16).ap()

        s_const = counter("s_const")
        s_const2 = counter("s_const2")
        s_x = [counter(f"s_x{i}") for i in range(NSC)]
        s_kout = [counter(f"s_kout{i}") for i in range(2 * NSC)]
        s_kin = [counter(f"s_kin{i}") for i in range(NSC)]
        s_qout = [counter(f"s_qout{i}") for i in range(2)]
        s_qin = [counter(f"s_qin{i}") for i in range(2)]
        s_minus = counter("s_minus")
        s_ow = counter("s_ow")
        s_mrows = counter("s_mrows")
        s_xload = counter("s_xload")
        s_store = counter("s_store")
        s_w = [counter(f"s_w{i}") for i in range(3)]
        s_pool = counter("s_pool")
        s_dve = counter("s_dve")
        s_act = counter("s_act")
        s_pe = counter("s_pe")
        s_max_scores = counter("s_max_scores")
        s_max = counter("s_max")
        s_scores = counter("s_scores")
        s_exp = counter("s_exp")
        s_pv = counter("s_pv")

        def pe(issue, sig=s_pe):
            return do("tensor", issue, sig)

        def matmul(o, lhsT, rhs, start=True, stop=True, sig=None):
            return do("tensor", lambda e: e.matmul(o, lhsT, rhs, start=start, stop=stop), sig)

        def transpose(o, i, eye, sig=None):
            return do("tensor", lambda e: e.transpose(o, i, eye), sig)

        def dve(issue, sig=s_dve):
            return do("vector", issue, sig)

        def act(o, i, func, bias=0.0, scale=1.0, sig=s_act):
            if func is None:
                return do("scalar", lambda e: e.copy(o, i), sig)
            return do("scalar", lambda e: e.activation(o, i, func, bias=bias, scale=scale), sig)

        def pool(issue, sig=s_pool):
            return do("gpsimd", issue, sig)

        def dma(o, i, sig):
            return do("sync", lambda e: e.dma_start(o, i), sig, by=16)

        banks = [p[:, :] for p in psum] + [w[:, j * BANK:(j + 1) * BANK] for w in wide for j in range(2)]
        free = {}
        lent = {"banks": [0, 1, 3], "next": 0}

        def borrow():
            i = lent["banks"][lent["next"] % len(lent["banks"])]
            lent["next"] += 1
            wait("tensor", free.get(i))
            return i, banks[i]

        def give_back(i, reader):
            free[i] = reader

        def load_slice(s):
            return dma(xs[s], x[s * SC:(s + 1) * SC, :].rearrange("(t p) c -> p t c", p=P), s_x[s])

        def contraction(matrix):
            return matrix.rearrange("(k p) c -> p k c", p=P)

        x_loaded = {0: load_slice(0)}
        for dst, src in ((ident[:, :], ident_f), (cw[:, :, :], contraction(conv_w)), (cb[:, :], conv_b),
                         (kw, contraction(k_wT)), (kb[:, :], k_b),
                         (vw, contraction(v_wT)), (vb_all[:, :], v_b.rearrange("(a c) -> a c", a=1).broadcast_to([P, C])),
                         (qw[:, :, :], contraction(q_wT)), (qb[:, :], q_b)):
            consts = dma(dst, src, s_const)
        for s in range(1, NSC):
            x_loaded[s] = load_slice(s)
        for dst, src in ((ob_all[:, :], o_b.rearrange("(a c) -> a c", a=1).broadcast_to([P, C])),
                         (fbT[:, :], fast_bT), (vlr[:, :], v_lr), (uTs, uT),
                         (gcol[:, :], gate.rearrange("(a c) -> a c", a=1).broadcast_to([R, 1]))):
            late_consts = dma(dst, src, s_const2)

        pool(lambda e: e.memset(half[:, :], -0.5))
        pool(lambda e: e.memset(xnT[:, :, 0:1], 0.0))
        pool(lambda e: e.memset(mparts[:, :, :], 0.0))
        pool_consts = pool(lambda e: e.memset(values[:, :, :, D:VW], 1.0))
        wait("gpsimd", pool_consts)
        m = pool(lambda e: e.memset(keys[SPLIT:ROWS, 0, :].bitcast(F32), MINUS_ONES))
        wait("gpsimd", m)
        wait("sync", m)
        minus_ones = dma(keys[SPLIT:ROWS, 1:H, :], keys[SPLIT:ROWS, 0:1, :].broadcast_to([PARTS, H - 1, NK]),
                         s_minus)
        pv_read = dve(lambda e: e.memset(pv_bank[:, :], 0.0))

        aggregated = [None]

        def layer_norm_stats(tiles, t0, ready, stats_read):
            at = slice(t0, t0 + len(tiles))
            wait("vector", ready, aggregated[0])
            for t, tokens in enumerate(tiles):
                mark = dve(lambda e, t=t, tokens=tokens: e.bn_stats(stats[:, t0 + t, :], tokens))
            wait("vector", mark, *stats_read)
            for t in range(t0, t0 + len(tiles)):
                mark = dve(lambda e, t=t: e.bn_aggr(meanvar[:, t, :], stats[:, t, :]))
            aggregated[0] = mark
            wait("gpsimd", mark, pool_consts, *stats_read)
            mark = pool(lambda e: e.tensor_scalar(rstd[:, at], meanvar[:, at, 1], LN_EPS, None, ALU.add))
            wait("gpsimd", mark)
            mark = pool(lambda e: e.tensor_tensor(rstd[:, at], rstd[:, at], half[:, at], ALU.pow))
            wait("gpsimd", mark)
            mark = pool(lambda e: e.tensor_tensor(shift[:, at], meanvar[:, at, 0], rstd[:, at], ALU.mult))
            wait("gpsimd", mark)
            return pool(lambda e: e.tensor_scalar(shift[:, at], shift[:, at], -1.0, None, ALU.mult))

        def normalise(engine, sig, dst, src, t):
            return do(engine, lambda e: e.tensor_scalar(dst, src, rstd[:, t:t + 1], shift[:, t:t + 1],
                                                        ALU.mult, ALU.add), sig)

        split_read = [{"full": None, "parts": None} for _ in split_sets]

        def split(which, bank, ready, bias, scale, engine, sig, store, store_sig, copier=None):
            copier, copier_sig = copier or (engine, sig)

            def rounding(dst, src):
                if copier == "scalar":
                    return lambda e: e.copy(dst, src)
                if copier == "gpsimd":
                    return lambda e: e.tensor_scalar(dst, src, 1.0, 1.0, ALU.mult, ALU.mult)
                return lambda e: e.tensor_copy(dst, src)

            i, b = bank
            whole_t, rest_t, parts = split_sets[which]
            read = split_read[which]
            wait("scalar", ready, read["full"])
            whole = act(whole_t, b, ACT.Identity, bias=bias, scale=scale)
            give_back(i, whole)
            wait(copier, whole, read["parts"])
            first = do(copier, rounding(parts[0], whole_t), copier_sig)
            wait(engine, first)
            m = do(engine, lambda e: e.tensor_tensor(rest_t, whole_t, parts[0], ALU.subtract), sig)
            wait(copier, m)
            second = do(copier, rounding(parts[1], rest_t), copier_sig)
            wait(engine, second)
            third = do(engine, lambda e: e.tensor_tensor(parts[2], rest_t, parts[1], ALU.subtract), sig)
            for j, mark in enumerate((first, second, third)):
                wait("sync", mark)
                stored = dma(store(j), parts[j], store_sig)
            read["full"], read["parts"] = third, stored
            return stored

        norm_ready = {}
        normalised = []
        xs_read = [None] * NSC
        xd_read, xd_ready = [None, None], [None, None]
        xnT_ready, k_ready = [], []

        def stats_of_slice(s):
            norm_ready[s] = layer_norm_stats([xs[s][:, t, :] for t in range(ST)], s * ST, x_loaded[s], ())

        def normalise_slice(s):
            wait("scalar", norm_ready[s])
            wait("gpsimd", norm_ready[s])
            for t in range(ST):
                tokens, col = xs[s][:, t, :], s * ST + t
                if t % 2:
                    mark = act(tokens, tokens, ACT.Identity, bias=shift[:, col:col + 1], scale=rstd[:, col:col + 1])
                else:
                    mark = normalise("gpsimd", s_pool, tokens, tokens, col)
                normalised.append(mark)

        def turn_slice(s):
            for half_slice in range(ST // QT):
                tiles = range(half_slice * QT, (half_slice + 1) * QT)
                wait("tensor", consts, *[normalised[s * ST + t] for t in tiles])
                for k in range(KC):
                    i, bank = borrow()
                    for j, t in enumerate(tiles):
                        m = transpose(bank[:, j * P:(j + 1) * P], xs[s][:, t, k * P:(k + 1) * P], ident[:, :], s_pe)
                    wait("scalar", m)
                    at = 1 + s * SC + half_slice * BANK
                    got = act(xnT[:, k, at:at + BANK], bank, None)
                    give_back(i, got)
            xs_read[s] = m
            xnT_ready.append(got)

        v_ready = None

        def convolve(s):
            xd = xds[s % 2]
            wait("vector", xnT_ready[s], xd_read[s % 2], consts, pool_consts)
            for k in range(KC):
                tap = [xnT[:, k, s * SC + i:s * SC + i + 2 * SK - 1:2] for i in range(3)]
                m = dve(lambda e, k=k, a=tap[1]: e.tensor_scalar(xd[:, k, :], a, cw[:, k, 1:2], cb[:, k:k + 1],
                                                                 ALU.mult, ALU.add))
                for i in (0, 2):
                    wait("vector", m)
                    m = dve(lambda e, k=k, i=i, a=tap[i]: e.scalar_tensor_tensor(
                        out=xd[:, k, :], in0=a, scalar=cw[:, k, i:i + 1], in1=xd[:, k, :],
                        op0=ALU.mult, op1=ALU.add))
            xd_ready[s % 2] = m

        def keys_of_slice(s):
            xd = xds[s % 2]
            wait("tensor", xd_ready[s % 2])
            for c in range(KC):
                bank = borrow()
                for k in range(KC):
                    m = matmul(bank[1], kw[:, k, c * P:(c + 1) * P], xd[:, k, :], start=(k == 0),
                               stop=(k == KC - 1), sig=s_pe)
                on_vector = c == 0 and s < 2
                engine, sig = ("vector", s_dve) if on_vector else ("gpsimd", s_pool)
                stored = split(c, bank, m, kb[:, c:c + 1], 1.0, engine, sig,
                               lambda j, c=c: k_parts[j, c * P:(c + 1) * P, s * SK:(s + 1) * SK], s_kout[2 * s + c],
                               copier=None if on_vector else ("scalar", s_act))
                wait("sync", stored)
                hs = c * (H // KC)
                for i, j in enumerate(K_PART):
                    m = dma(keys[i * D:(i + 1) * D, hs:hs + H // KC, s * SK:(s + 1) * SK],
                            k_parts[j, c * P:(c + 1) * P, s * SK:(s + 1) * SK].rearrange("(h d) n -> d h n", d=D),
                            s_kin[s])
            k_ready.append(m)

        def values_of_slice(s, beside=0):
            nonlocal v_ready
            xd = xds[s % 2]
            for pair in range(SK // P // 2):
                i, bank = borrow()
                for j in range(2):
                    if j:
                        early_maxima(beside)
                    o, kt = bank[:, j * C:(j + 1) * C], pair * 2 + j
                    for k in range(KC):
                        m = matmul(o, xd[:, k, kt * P:(kt + 1) * P], vw[:, k, :], start=(k == 0),
                                   stop=(k == KC - 1), sig=s_pe)
                xd_read[s % 2] = m
                kt = s * (SK // P) + pair * 2
                v = values[:, kt:kt + 2, :, 0:D]
                wait("scalar", m)
                m = act(v, bank.rearrange("p (t h d) -> p t h d", t=2, h=H), None)
                give_back(i, m)
                wait("gpsimd", m, consts)
                v_ready = pool(lambda e, v=v: e.tensor_tensor(
                    v, v, vb_all[:, :].rearrange("p (h d) -> p h d", d=D).unsqueeze(1).broadcast_to([P, 2, H, D]),
                    ALU.add))
                early_maxima(beside)

        q_ready = {}
        q_stored = {}
        scores_mark = {}
        q_rows_ready = {}
        unit = {"n": 0, "max": []}
        tile = {"n": 0, "exp": []}
        quad_done = []
        oT_read = attn_read = relu_read = mrows_read = None

        def queries_of(pair, engine="gpsimd", sig=s_pool, copier=None):
            c, hc, par, slot = pair // KC, pair % KC, pair % 2, (2 * pair) % SLOTS
            bank = borrow()
            wait("tensor", xnT_ready[c * CH // SC])
            for k in range(KC):
                m = matmul(bank[1], qw[:, k, hc * P:(hc + 1) * P], xnT[:, k, 1 + c * CH:1 + (c + 1) * CH],
                           start=(k == 0), stop=(k == KC - 1), sig=s_pe)
            wait("sync", q_ready.get(pair - 2))
            wait("scalar", qbs_ready)
            stored = split(0, bank, m, qbs[:, hc:hc + 1], SCALE, engine, sig,
                           lambda j: q_parts[par, j, :, :], s_qout[par], copier)
            wait("sync", stored, scores_mark.get(2 * pair - SLOTS + 1))
            for i, j in enumerate(Q_PART):
                m = dma(queries[i * D:(i + 1) * D, slot:slot + 2, :, :].rearrange("d b g n -> d (b g) n"),
                        q_parts[par, j, :, :].rearrange("(h d) n -> d h n", d=D), s_qin[par])
            q_ready[pair] = m

        def max_scores(b, q, g, at, j):
            n = unit["n"]
            bank = wide[n % 2]
            if b == 0:
                g, key_at, ready, over = g + j, at * SK, k_ready[at], slice_maxes[:, q, g:g + 2, at]
            else:
                key_at, ready, over = at * (NK // 2) + j * BANK, None, maxes[:, b % 2, q, g, at:at + 1]
            if j == 0:
                wait("tensor", q_ready[b // 2], ready)
                if n >= 2:
                    wait("tensor", unit["max"][n - 2])
            m = matmul(bank[:, j * BANK:(j + 1) * BANK], queries[0:SPLIT, b % SLOTS, g, q * P:(q + 1) * P],
                       keys[0:SPLIT, b % NG * G + g, key_at:key_at + BANK], sig=s_max_scores if j else None)
            if j == 1:
                unit["n"] += 1
                wait("vector", m, maxes_read[b % 2])
                read = bank[:, :].rearrange("p (j n) -> p j n", j=2) if b == 0 else bank[:, :]
                unit["max"].append(dve(lambda e: e.tensor_reduce(over, read, AX_X, ALU.max), s_max))

        oT_ready = attn_ready = None

        def max_units(b):
            if b == 0:
                return [(b, q, g, s, j) for s in range(NSC) for q in range(QT) for g in range(0, G, 2) for j in range(2)]
            return [(b, q, g, h, j) for q in range(QT) for g in range(G) for h in range(2) for j in range(2)]

        mparts_read = None
        maxes_read = [None, None]
        maxs_read = None

        def split_max(b):
            nonlocal maxs_read
            cols = mparts[:, :, :].rearrange("p t (g w) -> p t g w", g=G)
            mx = maxes[:, b % 2, :, :, :]
            wait("vector", unit["max"][-1], maxs_read)
            if b == 0:
                m = dve(lambda e: e.tensor_reduce(maxs[:, :, :], slice_maxes[:, :, :, :], AX_X, ALU.max))
            else:
                maxes_read[b % 2] = m = dve(lambda e: e.tensor_tensor(maxs[:, :, :], mx[:, :, :, 0], mx[:, :, :, 1],
                                                                      ALU.max))
            wait("gpsimd", mparts_read)
            left = maxs
            for j in range(PARTS):
                wait("gpsimd", m)
                m = pool(lambda e, j=j, a=left: e.tensor_scalar(cols[:, :, :, j], a[:, :, :], 1.0, 1.0,
                                                                ALU.mult, ALU.mult))
                if j < PARTS - 1:
                    wait("gpsimd", m)
                    m = pool(lambda e, j=j, a=left: e.tensor_tensor(maxr[:, :, :], a[:, :, :], cols[:, :, :, j],
                                                                    ALU.subtract))
                    left = maxr
            maxs_read = m
            return m

        def place_max(b, ready):
            nonlocal mparts_read
            i, bank = borrow()
            turned = bank[:, 0:BANK // 2].bitcast(BF16)
            wait("tensor", ready, identb_ready)
            for q in range(QT):
                m = transpose(turned[:, q * P:(q + 1) * P], mparts[:, q, :], identb[:, :], s_pe)
            mparts_read = m
            wait("scalar", m, q_rows_ready.get(b - 1, mrows_read))
            m = act(mrows[:, :], turned, None)
            give_back(i, m)
            wait("sync", m, scores_mark.get(b - SLOTS))
            for g in range(G):
                m = dma(queries[SPLIT:ROWS, b % SLOTS, g, :], mrows[32 * g:32 * g + PARTS, :], s_mrows)
            q_rows_ready[b] = m

        def score_tile(b, kt, g):
            n, head = tile["n"], b % NG * G + g
            tile["n"] += 1
            in_use = score_banks if b < NB - 1 else score_banks + [4, 5, 6, 7]
            i = in_use[n % len(in_use)]
            bank = banks[i]
            if kt == 0 and g == 0:
                wait("tensor", q_rows_ready[b], minus_ones)
            wait("tensor", free.get(i))
            m = matmul(bank, keys[0:ROWS, head, kt * P:(kt + 1) * P], queries[0:ROWS, b % SLOTS, g, :],
                       sig=s_scores)
            scores_mark[b] = m
            wait("scalar", m)
            if n < RING:
                wait("scalar", xs_read[n * CH // (ST * C)])
            else:
                wait("scalar", quad_done[n // G - 2])
            tile["exp"].append(act(probs[n % RING], bank, ACT.Exp, sig=s_exp))
            free[i] = tile["exp"][-1]

        def times_v(step):
            nonlocal pv_read
            b, kt = step // KT, step % KT
            wait("tensor", tile["exp"][G * step + G - 1], v_ready)
            if kt == 0:
                wait("tensor", pv_read)
            for g in range(G):
                m = matmul(pv_bank[32 * g:32 * g + VW, :], values[:, kt, b % NG * G + g, :],
                           probs[(G * step + g) % RING], start=(kt == 0), stop=(kt == KT - 1),
                           sig=s_pv if g == G - 1 else None)
            quad_done.append(m)

        def copy_sums():
            nonlocal pv_read, oT_ready
            wait("scalar", quad_done[-1], oT_read)
            oT_ready = pv_read = act(oT[:, :], pv_bank[:, :], None)

        def divide_sums(b):
            nonlocal oT_read, attn_ready
            i, bank = borrow()
            wait("tensor", oT_ready)
            for q in range(QT):
                m = transpose(bank[:, q * P:(q + 1) * P], oT[:, q * P:(q + 1) * P], ident[:, :], s_pe)
            oT_read = m
            sums = bank.rearrange("p (t g w) -> p t g w", t=QT, g=G)
            wait("vector", m, attn_read)
            m = dve(lambda e: e.reciprocal(rden[:, :, :], sums[:, :, :, D]))
            wait("vector", m)
            at = b % NG * G * D
            attn_ready = dve(lambda e: e.tensor_tensor(
                attn[:, :, at:at + G * D].rearrange("p t (g d) -> p t g d", g=G), sums[:, :, :, 0:D],
                rden[:, :, :].unsqueeze(3).broadcast_to([P, QT, G, D]), ALU.mult))
            give_back(i, attn_ready)

        w_ready = {}

        def ternary(w, t1, t2, wstat, ready, scaled=True):
            wait("gpsimd", ready)
            steps = [lambda e: e.tensor_scalar(t1, w, wstat[:, 1:2], None, ALU.is_gt),
                     lambda e: e.tensor_scalar(t2, w, wstat[:, 2:3], None, ALU.is_lt),
                     lambda e: e.tensor_tensor(t1, t1, t2, ALU.subtract),
                     lambda e: e.tensor_tensor(t1, t1, w, ALU.subtract),
                     lambda e: e.tensor_tensor(w, w, t1, ALU.add)]
            if scaled:
                steps.append(lambda e: e.tensor_scalar(w, w, wstat[:, 0:1], None, ALU.mult))
            for issue in steps:
                m = pool(issue)
                wait("gpsimd", m)
            return m

        def scales(w, width, wstat, ready, read):
            wait("vector", ready, read)
            m = dve(lambda e: e.tensor_reduce(wstat[:, 3:4], w, AX_X, ALU.add, apply_absolute_value=True))
            wait("vector", m)
            m = dve(lambda e: e.tensor_scalar(wstat[:, 0:1], wstat[:, 3:4], 1.0 / width, SCALE_MIN,
                                              ALU.mult, ALU.max))
            wait("vector", m)
            dve(lambda e: e.tensor_scalar(wstat[:, 1:2], wstat[:, 0:1], 0.5, None, ALU.mult))
            return dve(lambda e: e.tensor_scalar(wstat[:, 2:3], wstat[:, 0:1], -0.5, None, ALU.mult))

        def ffn_weights():
            i, bank = borrow()
            wait("tensor", late_consts)
            m = matmul(bank[0:R, 0:C], fbT[:, :], vlr[:, :], sig=s_pe)
            wait("vector", m, late_consts)
            low_ready = dve(lambda e: e.tensor_scalar(low[:, :], bank[0:R, 0:C], gcol[:, 0:1], None, ALU.mult))
            give_back(i, low_ready)
            AHEAD = 3
            tmp = [None] * AHEAD
            wstat_read = [None] * AHEAD

            t1, t2 = (r2[:, i * C:(i + 1) * C] for i in (AHEAD, AHEAD + 1))
            loaded, prepared = {}, {}

            def fc_tile(f):
                return r2[:, f % AHEAD * C:(f % AHEAD + 1) * C]

            def load_rows(f):
                if f < FT:
                    wait("sync", xd_read[0], xd_read[1], tmp[f % AHEAD])
                    loaded[f] = dma(fc_tile(f), w_fc[f * P:(f + 1) * P, :], s_w[f % AHEAD])

            def prepare_rows(f):
                if f < FT:
                    wstat = wstats[:, f % AHEAD, :]
                    ready = scales(fc_tile(f), C, wstat, loaded[f], wstat_read[f % AHEAD])
                    prepared[f] = wstat_read[f % AHEAD] = ternary(fc_tile(f), t1, t2, wstat, ready)

            for f in range(AHEAD):
                load_rows(f)
            yield
            for f in range(AHEAD - 1):
                prepare_rows(f)
            yield
            for f in range(FT):
                w = fc_tile(f)
                prepare_rows(f + AHEAD - 1)
                i, bank = borrow()
                wait("tensor", prepared[f], low_ready)
                for k in range(KC):
                    o = bank[:, k * P:(k + 1) * P]
                    matmul(o, w[:, k * P:(k + 1) * P], ident[:, :], start=True, stop=False)
                    m = matmul(o, low[:, k * P:(k + 1) * P], uTs[:, f * P:(f + 1) * P], start=False, stop=True,
                               sig=s_pe)
                tmp[f % AHEAD] = m
                load_rows(f + AHEAD)
                wait("scalar", m, xd_read[1])
                w_ready[1] = act(w1[:, :, f * P:(f + 1) * P],
                                 bank[:, 0:C].rearrange("p (k n) -> p k n", k=KC), None)
                give_back(i, w_ready[1])
                yield
            wide_w = r2[:, 0:F]
            for c in range(KC):
                wait("sync", *tmp)
                ready = dma(wide_w, w_proj[c * P:(c + 1) * P, :], s_w[c % 2])
                wstat = wstats[:, c, :]
                ready = scales(wide_w, F, wstat, ready, wstat_read[c])
                for h in range(2):
                    w = wide_w[:, h * BANK:(h + 1) * BANK]
                    m = ternary(w, r2[:, F:F + BANK], r2[:, F + BANK:F + 2 * BANK], wstat, ready,
                                scaled=False)
                    yield
                    if h == 0:
                        i, bank = borrow()
                        wait("tensor", ready)
                        m2 = matmul(bank[:, 0:P], wstat[:, 0:1].broadcast_to([P, P]), ident[:, :], sig=s_pe)
                        wait("scalar", m2)
                        w_ready[3] = act(w2_scale[:, c * P:(c + 1) * P], bank[:, 0:P], None)
                        give_back(i, w_ready[3])
                    yield
                    yield
                    i, bank = borrow()
                    wait("tensor", m)
                    for j in range(4):
                        m2 = transpose(bank[:, j * P:(j + 1) * P], w[:, j * P:(j + 1) * P], ident[:, :], s_pe)
                    wait("scalar", m2)
                    w_ready[2] = act(w2[:, 4 * h:4 * h + 4, c * P:(c + 1) * P],
                                     bank.rearrange("p (j n) -> p j n", j=4), None)
                    give_back(i, w_ready[2])
                tmp = [m2]
                yield
            r2_read[0] = m2

        r2_read = [None]
        state = {"stored": None, "attnT": None, "relu": None}

        def chunk_tail(c):
            nonlocal attn_read, stats_read, relu_read
            last = c == NCH - 1
            HT = QT // 2
            HN = HT * P
            elementwise, ew_sig = ("vector", s_dve) if last else ("gpsimd", s_pool)
            x2 = (ring if last else r2)[:, 0:QT * C].rearrange("p (t c) -> p t c", t=QT)
            halves = [b[:, :].bitcast(BF16).rearrange("p (j n) -> p j n", n=FT * HN) for b in (r2, w2_all, ring)]
            hidden = [[halves[0][:, 0, :], halves[0][:, 1, :], halves[1][:, 1, :]]] * 2
            if last:
                hidden[1] = [halves[2][:, 1 + j, :] for j in range(PARTS)]
            rows = out[c * CH:(c + 1) * CH, :].rearrange("(t p) c -> p t c", p=P)
            wait("sync", state["stored"] if c else w_ready[1])
            m = dma(x1[:, :, :], x[c * CH:(c + 1) * CH, :].rearrange("(t p) c -> p t c", p=P), s_xload)
            wait("gpsimd", m, late_consts)
            x1_ready = pool(lambda e: e.tensor_tensor(
                x1[:, :, :], x1[:, :, :], ob_all[:, :].unsqueeze(1).broadcast_to([P, QT, C]), ALU.add))

            def turn(src, ready, h):
                i, bank = borrow()
                wait("tensor", ready)
                for k in range(KC):
                    for q in range(HT):
                        at = k * HN + q * P
                        m = transpose(bank[:, at:at + P], src[:, h * HT + q, k * P:(k + 1) * P], ident[:, :], s_pe)
                wait("scalar", m, state["attnT"])
                got = act(attnT[:, :, h * HN:(h + 1) * HN], bank.rearrange("p (k n) -> p k n", k=KC), None)
                give_back(i, got)
                return m, got

            turned = [None, None]
            normed = [None, None]
            for h in range(2):
                attn_read, turned[h] = turn(attn, attn_ready, h)
                yield
            for h in range(2):
                i, bank = borrow()
                wait("tensor", turned[h], ow_ready)
                for j in range(HT):
                    q = HT * h + j
                    for k in range(KC):
                        m = matmul(bank[:, j * C:(j + 1) * C], attnT[:, k, q * P:(q + 1) * P], ow[:, k, :],
                                   start=(k == 0), stop=(k == KC - 1), sig=s_pe)
                state["attnT"] = m
                tiles = x1[:, HT * h:HT * (h + 1), :]
                wait("vector", m, x1_ready)
                m = dve(lambda e, tiles=tiles, bank=bank: e.tensor_tensor(
                    tiles, bank.rearrange("p (t c) -> p t c", t=HT), tiles, ALU.add))
                give_back(i, m)
                ready = layer_norm_stats([x1[:, q, :] for q in range(HT * h, HT * (h + 1))], HT * h, m, stats_read)
                wait(elementwise, ready, r2_read[0], quad_done[-1] if last else None)
                for q in range(HT * h, HT * (h + 1)):
                    normed[h] = normalise(elementwise, ew_sig, x2[:, q, :], x1[:, q, :], q)
                stats_read = (normed[h],)
                yield
            yield
            for h in range(2):
                _, turned[h] = turn(x2, normed[h], h)
                yield

            hidden_ready = [[], []]
            lanes = [(relu, elementwise, ew_sig, elementwise)]
            if last:
                lanes = [(relu, "vector", s_dve, "scalar"), (full, "vector", s_dve, "scalar"),
                         (oT, "gpsimd", s_pool, "gpsimd")]
            lane_read = [(relu_read,), (split_read[0]["full"],), (oT_read,)]

            def widen(units):
                marks = []
                for (h, fp), (buf, engine, sig, _), read in zip(units, lanes, lane_read):
                    i, bank = borrow()
                    wait("tensor", turned[h], w_ready[1])
                    for j in range(2):
                        f = 2 * fp + j
                        for k in range(KC):
                            m = matmul(bank[:, j * HN:(j + 1) * HN], w1[:, k, f * P:(f + 1) * P],
                                       attnT[:, k, h * HN:(h + 1) * HN], start=(k == 0), stop=(k == KC - 1),
                                       sig=s_pe)
                    state["attnT"] = m
                    wait("scalar", m, *read)
                    marks.append(act(buf[:, :], bank, ACT.Relu))
                    give_back(i, marks[-1])
                parts = [[p[:, fp * BANK:(fp + 1) * BANK] for p in hidden[h]] for h, fp in units]
                for u, (buf, engine, sig, _) in enumerate(lanes[:len(units)]):
                    wait(engine, marks[u])
                    marks[u] = do(engine, lambda e, b=buf: e.tensor_tensor(b[:, :], b[:, :], b[:, :], ALU.mult), sig)
                    wait(engine, r2_read[0])
                for j in range(PARTS - 1):
                    for u, (buf, engine, sig, copier) in enumerate(lanes[:len(units)]):
                        dst = parts[u][j]
                        wait(copier, marks[u])
                        if copier == "scalar":
                            marks[u] = act(dst, buf[:, :], None)
                        else:
                            marks[u] = do(copier, lambda e, d=dst, b=buf: e.tensor_scalar(
                                d, b[:, :], 1.0, 1.0, ALU.mult, ALU.mult), sig)
                    for u, (buf, engine, sig, _) in enumerate(lanes[:len(units)]):
                        left = buf[:, :] if j < PARTS - 2 else parts[u][PARTS - 1]
                        wait(engine, marks[u])
                        marks[u] = do(engine, lambda e, l=left, b=buf, d=parts[u][j]: e.tensor_tensor(
                            l, b[:, :], d, ALU.subtract), sig)
                for u, (h, _) in enumerate(units):
                    lane_read[u] = (marks[u],)
                    hidden_ready[h].append(marks[u])

            def narrow(h):
                i, bank = borrow()
                wait("tensor", *hidden_ready[h], w_ready[2])
                for j in range(HT):
                    for f in range(FT):
                        at = f * HN + j * P
                        for p, part_p in enumerate(hidden[h]):
                            m = matmul(bank[:, j * C:(j + 1) * C], part_p[:, at:at + P], w2[:, f, :],
                                       start=(f == 0 and p == 0), stop=(f == FT - 1 and p == PARTS - 1), sig=s_pe)
                r2_read[0] = m
                tiles = x1[:, HT * h:HT * (h + 1), :]
                wait("vector", m, w_ready[3])
                product = bank.rearrange("p (t c) -> p t c", t=HT)
                m = dve(lambda e: e.tensor_tensor(
                    product, product, w2_scale[:, :].unsqueeze(1).broadcast_to([P, HT, C]), ALU.mult))
                wait("vector", m)
                m = dve(lambda e, tiles=tiles, bank=bank: e.tensor_tensor(
                    tiles, bank.rearrange("p (t c) -> p t c", t=HT), tiles, ALU.add))
                give_back(i, m)
                wait("sync", m)
                state["stored"] = dma(rows[:, HT * h:HT * (h + 1), :], tiles, s_store)

            if last:
                units = [(h, fp) for h in range(2) for fp in range(FT // 2)]
                for u in range(0, len(units), len(lanes)):
                    widen(units[u:u + len(lanes)])
                narrow(0)
                narrow(1)
            else:
                for h in range(2):
                    for fp in range(FT // 2):
                        widen([(h, fp)])
                        yield
                    narrow(h)
                    yield
            relu_read = lane_read[0][0]

        units = [u for b in range(NB) for u in max_units(b)]
        per_step = len(max_units(0)) // KT
        stats_of_slice(0)
        wait("vector", consts)
        identb_ready = dve(lambda e: e.tensor_copy(identb[:, :], ident[:, :]))
        qbs_ready = dve(lambda e: e.tensor_scalar(qbs[:, :], qb[:, :], SCALE, None, ALU.mult))
        of_slice = per_step * KT // NSC
        early = 0

        def early_maxima(share):
            nonlocal early
            for u in units[early:early + share]:
                max_scores(*u)
            early += share

        normalise_slice(0)
        stats_of_slice(1)
        turn_slice(0)
        normalise_slice(1)
        stats_of_slice(2)
        convolve(0)
        turn_slice(1)
        normalise_slice(2)
        keys_of_slice(0)
        stats_of_slice(3)
        convolve(1)
        queries_of(0, "vector", s_dve, ("scalar", s_act))
        normalise_slice(3)
        values_of_slice(0)
        turn_slice(2)
        keys_of_slice(1)
        convolve(2)
        values_of_slice(1)
        turn_slice(3)
        convolve(3)
        keys_of_slice(2)
        early_maxima(of_slice // 2)
        keys_of_slice(3)
        early_maxima(of_slice // 2)
        for s in range(2, NSC):
            values_of_slice(s, of_slice * P // SK)
        stats_read = normalised[-2:]
        lent["banks"], lent["next"] = [3], 0
        wait("sync", split_read[1]["full"], split_read[1]["parts"])
        ow_ready = dma(ow[:, :, :], contraction(o_wT), s_ow)
        oT_read, relu_read, mrows_read = (split_read[1]["full"],) * 2 + (split_read[1]["parts"],)
        stage = ffn_weights()
        for _ in range(2):
            next(stage)
        taken = per_step * KT
        early_maxima(taken - early)
        parts0 = split_max(0)
        early_maxima(per_step)
        place_max(0, parts0)
        early_maxima(2 * per_step)
        taken = early
        for step in range(NB * KT + 1):
            b, kt = step // KT, step % KT
            if step == (NB - 1) * KT:
                free.update({i: unit["max"][-1] for i in range(4, 8)})
            if b < NB:
                target = min(per_step * (step + 1 + KT + LEAD),
                             early + -(-(2 * per_step * KT - early) * (step + 1) // (KT - LEAD)))
                later = units[taken:target]
                taken = target
                score_tile(b, kt, 0)
                score_tile(b, kt, 1)
                for u in later[:3]:
                    max_scores(*u)
                score_tile(b, kt, 2)
                for u in later[3:]:
                    max_scores(*u)
                score_tile(b, kt, 3)
                if kt == KT - LEAD - 1 and b + 1 < NB:
                    parts = split_max(b + 1)
                if kt == KT - LEAD + 1 and b + 1 < NB:
                    place_max(b + 1, parts)
                if kt == 1 and b % 2 == 0 and b + 2 < NB:
                    queries_of(b // 2 + 1)
                if kt == 2 and b > 0:
                    divide_sums(b - 1)
                if kt in (3, 5, 7, 9, 11, 15):
                    if kt == 3 and b % NG == 0 and b > 0:
                        for _ in stage:
                            pass
                        stage = chunk_tail(b // NG - 1)
                    next(stage, None)
            if step > 0:
                times_v(step - 1)
                if step % KT == 0:
                    copy_sums()
        lent["banks"], lent["next"] = [3, 0, 1, 4, 5, 6, 7], 0
        divide_sums(NB - 1)
        for _ in chunk_tail(NCH - 1):
            pass
        for s in s_kout + s_qout + [s_store]:
            wait("sync", (s["sem"], s["count"]))

        with nc.Block() as block:
            @block.tensor
            def _(e):
                issue_all("tensor", e)

            @block.vector
            def _(e):
                issue_all("vector", e)

            @block.scalar
            def _(e):
                issue_all("scalar", e)

            @block.gpsimd
            def _(e):
                issue_all("gpsimd", e)

            @block.sync
            def _(e):
                issue_all("sync", e)


def kernel(**inputs):
    import numpy as np
    import concourse.bacc as bacc
    from concourse.bass_utils import run_bass_kernel_spmd

    def get(name):
        return np.asarray(inputs[name])

    def by_partition(name):
        return get(name).reshape(-1, P).T

    x = get("L0_attn_x")
    arrays = {
        "x": x.reshape(x.shape[1:]),
        "q_wT": get("L0_attn_q_w").T, "q_b": by_partition("L0_attn_q_b"),
        "k_wT": get("L0_attn_k_w").T, "k_b": by_partition("L0_attn_k_b"),
        "v_wT": get("L0_attn_v_w").T, "v_b": get("L0_attn_v_b"),
        "conv_w": get("L0_attn_conv_w").reshape(x.shape[2], -1), "conv_b": by_partition("L0_attn_conv_b"),
        "o_wT": get("L0_attn_out_w").T, "o_b": get("L0_attn_out_b"),
        "fast_bT": get("L0_ffn_fast_b").T,
        "w_fc": get("L0_ffn_w_fc"), "w_proj": get("L0_ffn_w_proj"),
        "uT": get("L0_ffn_u").T, "v_lr": get("L0_ffn_v"), "gate": get("L0_ffn_gate").reshape(1),
        "ident_f": np.eye(P, dtype=np.float32),
    }
    arrays = {name: np.ascontiguousarray(a) for name, a in arrays.items()}
    nc = bacc.Bacc("TRN2", target_bir_lowering=False, num_devices=1)
    args = [nc.dram_tensor(name, a.shape, mybir.dt.from_np(a.dtype), kind="ExternalInput").ap()
            for name, a in arrays.items()]
    out = nc.dram_tensor("out", arrays["x"].shape, F32, kind="ExternalOutput").ap()
    build_layer(nc, *args, out)
    result = run_bass_kernel_spmd(nc, [arrays], core_ids=[0])
    return result.results[0]["out"].reshape(x.shape)
```
